# Optimizing a Trainium2 kernel written in Bass

```python
import numpy as np
import jax
import jax.numpy as jnp

def _softmax(x, axis=-1):
    return jax.nn.softmax(x, axis=axis)

def _gelu(x):
    return jax.nn.gelu(x, approximate=True)

def _silu(x):
    return jax.nn.silu(x)

def _sigmoid(x):
    return jax.nn.sigmoid(x)

def _layernorm(x, axis=-1, eps=1e-05):
    m = jnp.mean(x, axis=axis, keepdims=True)
    v = jnp.var(x, axis=axis, keepdims=True)
    return (x - m) / jnp.sqrt(v + eps)

def _scatter_add(tgt, idx, src, axis=0):
    return tgt.at[idx].add(src)

def _segment_sum(src, seg, n):
    return jax.ops.segment_sum(src, seg, n)
kernel_name = 'mk_vit_tower_d1_tok_img1024_r4_a5115e'

def setup_inputs(seed: int=0):
    np.random.seed(seed)
    _w = jnp.asarray

    def _rec_inputs():
        import jax
        import jax.numpy as jnp
        _rk = jax.random.key(seed)
        x = -0.00016672 + 0.999947 * jax.random.normal(jax.random.fold_in(_rk, 1), (64, 3, 96, 96), jnp.float32)
        return x
    x = _rec_inputs()

    def _L0_tok_setup():
        import jax, jax.numpy as jnp
        import numpy as np
        IMG = 96
        P = 16
        C = 3
        D = 256
        B = 64
        key = jax.random.key(seed)
        kx, kw, kb = jax.random.split(key, 3)
        fan_in = C * P * P
        bound = 1.0 / np.sqrt(fan_in)
        x = jax.random.normal(kx, (B, C, IMG, IMG), dtype=jnp.float32)
        W = jax.random.uniform(kw, (D, fan_in), dtype=jnp.float32, minval=-bound, maxval=bound)
        b = jax.random.uniform(kb, (D,), dtype=jnp.float32, minval=-bound, maxval=bound)
        return {'x': x, 'W': W, 'b': b}
    _L0_tok_all = _L0_tok_setup()
    _L0_tok_in = {k: v for k, v in _L0_tok_all.items() if k in ('W', 'b')}
    del _L0_tok_all

    def _L0_attn_setup():
        import jax, jax.numpy as jnp
        import numpy as np
        LN_EPS = 1e-05
        NUM_HEAD = 16
        key = jax.random.key(seed)
        ks = jax.random.split(key, 10)
        B, S, E = (2, 512, 256)
        sc = 0.02
        return {'x': jax.random.normal(ks[0], (B, S, E), jnp.float32), 'wq': jax.random.normal(ks[1], (E, E), jnp.float32) * sc, 'bq': jax.random.normal(ks[2], (E,), jnp.float32) * sc, 'wk': jax.random.normal(ks[3], (E, E), jnp.float32) * sc, 'bk': jax.random.normal(ks[4], (E,), jnp.float32) * sc, 'wv': jax.random.normal(ks[5], (E, E), jnp.float32) * sc, 'bv': jax.random.normal(ks[6], (E,), jnp.float32) * sc, 'wo': jax.random.normal(ks[7], (E, E), jnp.float32) * sc, 'bo': jax.random.normal(ks[8], (E,), jnp.float32) * sc, 'gamma': jnp.ones((E,), jnp.float32), 'beta': jnp.zeros((E,), jnp.float32)}
    _L0_attn_all = _L0_attn_setup()
    _L0_attn_in = {k: v for k, v in _L0_attn_all.items() if k in ('wq', 'bq', 'wk', 'bk', 'wv', 'bv', 'wo', 'bo', 'gamma', 'beta')}
    del _L0_attn_all

    def _L0_ffn_setup():
        import jax, jax.numpy as jnp
        import numpy as np
        NUM_EXPERTS = 8
        EXPERT_CAPACITY = 2.0
        key = jax.random.key(seed)
        k1, k2, k3, k4 = jax.random.split(key, 4)
        B, T, C, H, E = (4, 1024, 256, 1024, NUM_EXPERTS)
        x = jax.random.normal(k1, (B, T, C), jnp.float32)
        gate_w = jax.random.normal(k2, (C, E), jnp.float32) * 0.02
        w1 = jax.random.normal(k3, (E, C, H), jnp.float32) * 0.02
        w2 = jax.random.normal(k4, (E, H, C), jnp.float32) * 0.02
        return {'x': x, 'gate_w': gate_w, 'w1': w1, 'w2': w2}
    _L0_ffn_all = _L0_ffn_setup()
    _L0_ffn_in = {k: v for k, v in _L0_ffn_all.items() if k in ('gate_w', 'w1', 'w2')}
    del _L0_ffn_all
    return {'x': x, 'L0_tok_W': _L0_tok_in['W'], 'L0_tok_b': _L0_tok_in['b'], 'L0_attn_wq': _L0_attn_in['wq'], 'L0_attn_bq': _L0_attn_in['bq'], 'L0_attn_wk': _L0_attn_in['wk'], 'L0_attn_bk': _L0_attn_in['bk'], 'L0_attn_wv': _L0_attn_in['wv'], 'L0_attn_bv': _L0_attn_in['bv'], 'L0_attn_wo': _L0_attn_in['wo'], 'L0_attn_bo': _L0_attn_in['bo'], 'L0_attn_gamma': _L0_attn_in['gamma'], 'L0_attn_beta': _L0_attn_in['beta'], 'L0_ffn_gate_w': _L0_ffn_in['gate_w'], 'L0_ffn_w1': _L0_ffn_in['w1'], 'L0_ffn_w2': _L0_ffn_in['w2']}

def reference(x, L0_tok_W, L0_tok_b, L0_attn_wq, L0_attn_bq, L0_attn_wk, L0_attn_bk, L0_attn_wv, L0_attn_bv, L0_attn_wo, L0_attn_bo, L0_attn_gamma, L0_attn_beta, L0_ffn_gate_w, L0_ffn_w1, L0_ffn_w2):
    import jax
    import jax.numpy as jnp

    def _L0_tok_ref(x, W, b):
        import jax, jax.numpy as jnp
        import numpy as np
        IMG = 96
        P = 16
        C = 3
        D = 256
        B = 64
        Bsz, Cc, H, Wd = x.shape
        gh, gw = (H // P, Wd // P)
        patches = x.reshape(Bsz, Cc, gh, P, gw, P).transpose(0, 2, 4, 1, 3, 5)
        patches = patches.reshape(Bsz, gh * gw, Cc * P * P)
        return jnp.einsum('bnf,df->bnd', patches, W) + b

    def _L0_attn_ref(x, wq, bq, wk, bk, wv, bv, wo, bo, gamma, beta):
        import jax, jax.numpy as jnp
        import numpy as np
        LN_EPS = 1e-05
        NUM_HEAD = 16
        B, S, E = x.shape
        H = NUM_HEAD
        D = E // H
        Q = x @ wq + bq
        K = x @ wk + bk
        V = x @ wv + bv
        Q = Q.reshape(B * H, S, D)
        K = K.reshape(B * H, S, D)
        V = V.reshape(B * H, S, D)
        scores = jnp.einsum('bqd,bkd->bqk', Q, K) / jnp.sqrt(jnp.float32(D))
        attn = jax.nn.softmax(scores, axis=-1)
        ctx = jnp.einsum('bqk,bkd->bqd', attn, V)
        ctx = ctx.reshape(B, S, E)
        out = ctx @ wo + bo
        out = out + x
        mu = jnp.mean(out, axis=-1, keepdims=True)
        var = jnp.var(out, axis=-1, keepdims=True)
        out = (out - mu) * jax.lax.rsqrt(var + LN_EPS) * gamma + beta
        return out

    def _L0_ffn_ref(x, gate_w, w1, w2):
        import jax, jax.numpy as jnp
        import numpy as np
        NUM_EXPERTS = 8
        EXPERT_CAPACITY = 2.0
        B, T, C = x.shape
        E = gate_w.shape[1]
        cap = int(EXPERT_CAPACITY * T / E)
        scores = jnp.einsum('BTC,CE->BTE', x, gate_w)
        probs = jax.nn.softmax(scores, axis=-1)
        probs_et = jnp.transpose(probs, (0, 2, 1))
        top_p, top_idx = jax.lax.top_k(probs_et, cap)
        xin = jnp.take_along_axis(x[:, None, :, :], top_idx[..., None], axis=2)
        h = jax.nn.gelu(jnp.einsum('BElC,ECH->BElH', xin, w1), approximate=False)
        y = jnp.einsum('BElH,EHC->BElC', h, w2)
        y = y * top_p[..., None]
        b_idx = jnp.arange(B)[:, None, None]
        out = jnp.zeros((B, T, C), x.dtype).at[b_idx, top_idx].add(y)
        return out
    h = _L0_tok_ref(x, L0_tok_W, L0_tok_b)
    h = h + _L0_attn_ref(_layernorm(h, axis=-1), L0_attn_wq, L0_attn_bq, L0_attn_wk, L0_attn_bk, L0_attn_wv, L0_attn_bv, L0_attn_wo, L0_attn_bo, L0_attn_gamma, L0_attn_beta)
    h = h + _L0_ffn_ref(_layernorm(h, axis=-1), L0_ffn_gate_w, L0_ffn_w1, L0_ffn_w2)
    return h

_drawn_inputs = setup_inputs


def setup_inputs(seed=0):
    import zlib

    import numpy as np

    out = dict(_drawn_inputs(seed))
    spreads = {'L0_attn_gamma': (1.0, 0.2), 'L0_attn_beta': (0.0, 0.1)}
    factors = {'L0_attn_wq': 8.0,
     'L0_attn_bq': 8.0,
     'L0_attn_wk': 8.0,
     'L0_attn_bk': 8.0,
     'L0_attn_wv': 5.237,
     'L0_attn_bv': 8.0,
     'L0_attn_wo': 5.009,
     'L0_attn_bo': 4.436,
     'L0_ffn_gate_w': 3.791,
     'L0_ffn_w1': 3.341,
     'L0_ffn_w2': 3.267}
    for name, (base, spread) in spreads.items():
        noise = np.random.default_rng([zlib.crc32(name.encode()), seed]).standard_normal(out[name].shape)
        drawn = base * np.exp(spread * noise) if base else spread * noise
        out[name] = jnp.asarray(drawn.astype(out[name].dtype))
    for name, factor in factors.items():
        out[name] = (out[name] * factor).astype(out[name].dtype)
    return out
```

```python
from contextlib import ExitStack

import numpy as np

import concourse.bass as bass
from concourse import mybir

F32 = mybir.dt.float32
ALU = mybir.AluOpType
ACT = mybir.ActivationFunctionType
AX = mybir.AxisListType.X

P = 128
B, C, IMG, PATCH = 64, 3, 96, 16
G = IMG // PATCH
N = G * G
D = 256
KD = D // P
KF = C * PATCH * PATCH // P
HEADS, HD = 16, 16
E, CAP = 8, 2 * N // 8
HID = 1024
KH = HID // P
UB = 6
UT = UB * N
NU = -(-B // UB)
LASTB = B - (NU - 1) * UB
TT = 3 * N
T = NU * UT
SLOTS = B * CAP
PSLOTS = NU * UB * CAP
TS = 3 * CAP
IC = 8 * N
LN_EPS = 1e-5

M_ID = 0
M_BLK = M_ID + P
M_IND = M_BLK + TT
M_I36 = M_IND + TT
M_LOW = M_I36 + N
M_IOTA = M_LOW + N
M_OBD = M_IOTA + TS
M_IND96 = M_OBD + 96
M_END = M_IND96 + 96


def shape_masks():
    m = np.zeros((P, M_END), np.float32)
    t = np.arange(TT)
    m[:, M_ID:M_ID + P] = np.eye(P)
    m[:TT, M_BLK:M_BLK + TT] = (t[:, None] // N) == (t[None, :] // N)
    m[:3, M_IND:M_IND + TT] = np.arange(3)[:, None] == (t[None, :] // N)
    m[:TT, M_I36:M_I36 + N] = (t[:, None] % N) == np.arange(N)[None, :]
    m[:TT, M_LOW:M_LOW + N] = np.arange(N)[None, :] < (t[:, None] % N)
    s = np.arange(TS)
    m[:TT, M_IOTA:M_IOTA + TS] = np.where(s[None, :] // CAP == t[:, None] // N, s[None, :] % CAP, -1)
    q = np.arange(96)
    m[:TT, M_OBD:M_OBD + 96] = (t[:, None] // N) == (q[None, :] // 32)
    m[:3, M_IND96:M_IND96 + 96] = np.arange(3)[:, None] == (q[None, :] // 32)
    return m


def over_units(eng, body):
    for i in range(2):
        body(i, i, 1)
    with eng.Fori(0, (NU - 5) // 2) as p:
        body(p * 2 + 2, 0, p + 2)
        body(p * 2 + 3, 1, p + 2)
    for i in range(NU - 3, NU):
        body(i, i % 2, i // 2 + 1)


def build(nc, x, tok_w, tok_b, wq, bq, wk, bk, wv, bv, wo, bo, gamma, beta, gate_w, w1, w2, masks, out):
    def dram(name, shape):
        return nc.dram_tensor(name, shape, F32).ap()

    qT_d = dram("qT_scratch", [D, T])
    kT_d = dram("kT_scratch", [D, T])
    v_d = dram("v_scratch", [T, D])
    cT_d = dram("cT_scratch", [D, T])
    spt_d = dram("spt_scratch", [NU * 2, TT, 2 * TT])
    q_view = qT_d.rearrange("(j d) t -> d j t", d=HD)
    k_view = kT_d.rearrange("(j d) t -> d j t", d=HD)
    c_view = cT_d.rearrange("(j d) t -> d j t", d=HD)
    v_flat = v_d.rearrange("t e -> (t e)")

    top = ExitStack()
    with top:
        def sem(name):
            return top.enter_context(nc.semaphore(name))

        def sb(ctx, name, shape):
            return ctx.enter_context(nc.sbuf_tensor(name, shape, F32))

        def psum(ctx, name):
            return ctx.enter_context(nc.psum_tensor(name, [P, 512], F32))

        bank = [psum(top, f"bank{i}") for i in range(8)]
        mk = sb(top, "mk", [P, M_END])
        ident = mk[:, M_ID:M_ID + P]
        colb = sb(top, "colb", [P, 3, KD])
        rowb = sb(top, "rowb", [TT, 4, D])
        wo_s = sb(top, "wo_s", [P, KD, D])
        gate_s = sb(top, "gate_s", [P, KD, E])
        nh = sb(top, "nh", [TT, 2])
        hb = sb(top, "hb", [TT, 2 * NU, D])
        x1b = sb(top, "x1b", [TT, 2 * NU, D])
        s_const = sem("const_in")

        s_parted = sem("waits_parted")

        def part_waits(eng):
            eng.sem_inc(s_parted, 1)

        bv_bc, bo_bc, ga_bc, be_bc = (rowb[:, k, :] for k in range(4))

        def two(ap):
            return ap.unsqueeze(1).to_broadcast([TT, 2, D])

        s_wts = sem("weights_in")
        s_x = [sem("x_in0"), sem("x_in1")]
        s_wTt, s_wTc = sem("wT_transposed"), sem("wT_copied")
        s_hve = sem("h_var_eps")
        s_nh = sem("minus_half")
        s_xr = sem("pixels_regrouped")
        s_pT, s_pTc = sem("patches_transposed"), sem("patches_copied")
        s_hT, s_hTc = sem("hT_done"), sem("hT_copied")
        s_h, s_hbn, s_hag, s_hrs, s_x1, s_hb = (sem(n) for n in ("h_done", "h_bn", "h_aggr", "h_rstd", "x1_done", "hb_done"))
        s_x1b = sem("x1b_done")
        s_x1T, s_x1Tc = sem("x1T_done"), sem("x1T_copied")
        s_qk, s_qkc, s_v, s_vc = sem("qk_done"), sem("qk_copied"), sem("v_done"), sem("v_copied")
        s_qkst, s_vst = sem("qk_stored"), sem("v_stored")
        s_bq4 = sem("bq_scaled")

        with ExitStack() as ctx, nc.allow_non_contiguous_dma(reason="bias columns"):
            xraw = [sb(ctx, f"xraw{k}", [UB * G, C, PATCH * IMG]) for k in range(2)]
            xr = sb(ctx, "xr", [UB * G, C, G, PATCH * PATCH])
            wnat = sb(ctx, "wnat", [P, KD, C * PATCH * PATCH])
            wT = sb(ctx, "wT", [P, KF, D])
            wq_s, wk_s, wv_s = (sb(ctx, n, [P, KD, D]) for n in ("wq_s", "wk_s", "wv_s"))
            pT = sb(ctx, "pT", [P, KF, UT])
            hTs = sb(ctx, "hTs", [P, KD, UT])
            x1s = sb(ctx, "x1s", [TT, 2, D])
            x1Ts = sb(ctx, "x1Ts", [P, KD, UT])
            qs = sb(ctx, "qs", [P, KD, UT])
            ks = sb(ctx, "ks", [P, KD, UT])
            vs = sb(ctx, "vs", [TT, 2, D])
            st = sb(ctx, "st", [TT, 2, 6])
            mv = sb(ctx, "mv", [TT, 2, 2])
            rs = sb(ctx, "rs", [TT, 2])
            ve = sb(ctx, "ve", [TT, 2])
            hT_ps, h_ps, x1T_ps, q_ps, k_ps, v_ps = bank[3], bank[4], bank[5], bank[6], bank[7], bank[3]

            with nc.Block() as block:
                @block.sync
                def _(sp):
                    def load_x(i, par):
                        nb = LASTB if isinstance(i, int) and i == NU - 1 else UB
                        for c in range(C):
                            src = x[bass.ds(i * UB, nb), c, :, :].rearrange("b (g r) w -> b g (r w)", g=G)
                            sp.dma_start(xraw[par][0:nb * G, c, :], src).then_inc(s_x[par], 16)

                    load_x(0, 0)
                    sp.dma_start(mk[:], masks).then_inc(s_const, 16)
                    sp.dma_start(wnat[:], tok_w.rearrange("(h p) f -> p h f", p=P)).then_inc(s_const, 16)
                    load_x(1, 1)
                    for k, v in enumerate((tok_b, bq, bk)):
                        sp.dma_start(colb[:, k, :], v.rearrange("(h p) -> p h", p=P)).then_inc(s_wts, 16)
                    for k, v in enumerate((bv, bo, gamma, beta)):
                        sp.dma_start(rowb[:, k, :], v.partition_broadcast(TT)).then_inc(s_wts, 16)
                    for dst, v in ((wq_s, wq), (wk_s, wk), (wv_s, wv), (wo_s, wo), (gate_s, gate_w)):
                        sp.dma_start(dst[:], v.rearrange("(k p) n -> p k n", p=P)).then_inc(s_wts, 16)

                    def body(i, par, uses):
                        last = isinstance(i, int) and i >= NU - 2
                        sp.wait_ge(s_xr, (i + 1) * C)
                        if not last:
                            load_x(i + 2, par)
                        sp.wait_ge(s_qkc, (i + 1) * 4)
                        sp.dma_start(qT_d.rearrange("(h p) t -> p h t", p=P)[:, :, bass.ds(i * UT, UT)], qs[:]).then_inc(s_qkst, 16)
                        sp.dma_start(kT_d.rearrange("(h p) t -> p h t", p=P)[:, :, bass.ds(i * UT, UT)], ks[:]).then_inc(s_qkst, 16)
                        sp.wait_ge(s_vc, i + 1)
                        sp.dma_start(v_d[bass.ds(i * UT, UT), :].rearrange("(u t) e -> t u e", u=2), vs[:]).then_inc(s_vst, 16)

                    over_units(sp, body)
                    sp.wait_ge(s_qkst, 32 * NU)
                    sp.wait_ge(s_vst, 16 * NU)

                @block.gpsimd
                def _(pool):
                    def regroup(i, par, uses):
                        pool.wait_ge(s_x[par], uses * 16 * C)
                        pool.wait_ge(s_pT, i * KF)
                        part_waits(pool)
                        for c in range(C):
                            nc.gpsimd.tensor_copy(xr[:, c].rearrange("p g (r w) -> p g r w", w=PATCH),
                                                  xraw[par][:, c].rearrange("p (r g w) -> p g r w", g=G, w=PATCH)).then_inc(s_xr, 1)

                    nc.gpsimd.memset(nh[:], -0.5).then_inc(s_nh, 1)
                    regroup(0, 0, 1)
                    pool.wait_ge(s_nh, 1)
                    pool.wait_ge(s_wts, 12 * 16)

                    def body(i, par, uses):
                        if not (isinstance(i, int) and i == NU - 1):
                            regroup(i + 1, 1 - par, uses + par)
                        pool.wait_ge(s_hve, i + 1)
                        nc.gpsimd.tensor_tensor(rs[:], ve[:], nh[:], ALU.pow).then_inc(s_hrs, 1)
                        pool.wait_ge(s_x1, i + 1)
                        nc.gpsimd.tensor_tensor(x1b[:, bass.ds(i * 2, 2), :], x1s[:], two(bo_bc), ALU.add).then_inc(s_x1b, 1)
                    over_units(pool, body)

                @block.tensor
                def _(pe):
                    pe.wait_ge(s_const, 32)
                    for k in range(KF):
                        for h in range(KD):
                            last = nc.tensor.transpose(bank[k // 2][:, (k % 2) * D + h * P:(k % 2) * D + (h + 1) * P],
                                                       wnat[:, h, k * P:(k + 1) * P], ident)
                    last.then_inc(s_wTt, 1)
                    pe.wait_ge(s_wTc, 3)

                    def patches(i, par, uses):
                        pe.wait_ge(s_xr, (i + 1) * C)
                        pe.wait_ge(s_pTc, i * 3)
                        part_waits(pe)
                        for k in range(KF):
                            for g in range(G):
                                o = (k % 2) * UT + g * UB * G
                                last = nc.tensor.transpose(bank[k // 2][:, o:o + UB * G],
                                                           xr[:, k // 2, g, (k % 2) * P:(k % 2 + 1) * P],
                                                           ident[0:UB * G, 0:UB * G])
                            last.then_inc(s_pT, 1)

                    def body(i, par, uses):
                        pe.wait_ge(s_pTc, (i + 1) * 3)
                        pe.wait_ge(s_vc, i)
                        for h in range(KD):
                            for k in range(KF):
                                last = nc.tensor.matmul(hT_ps[:, h * UT:(h + 1) * UT], wT[:, k, h * P:(h + 1) * P],
                                                        pT[:, k, :], start=(k == 0), stop=(k == KF - 1))
                        last.then_inc(s_hT, 1)
                        if not (isinstance(i, int) and i == NU - 1):
                            patches(i + 1, 1 - par, uses + par)
                        pe.wait_ge(s_hTc, (i + 1) * 2)
                        pe.wait_ge(s_hb, i)
                        pe.wait_ge(s_x1, i)
                        for u in range(2):
                            for h in range(KD):
                                last = nc.tensor.transpose(h_ps[0:TT, u * D + h * P:u * D + (h + 1) * P],
                                                           hTs[:, h, u * TT:(u + 1) * TT], ident)
                        last.then_inc(s_h, 1)
                        pe.wait_ge(s_x1, i + 1)
                        pe.wait_ge(s_x1Tc, i)
                        for h in range(KD):
                            for u in range(2):
                                last = nc.tensor.transpose(x1T_ps[:, h * UT + u * TT:h * UT + (u + 1) * TT],
                                                           x1s[:, u, h * P:(h + 1) * P], ident[0:TT, 0:TT])
                        last.then_inc(s_x1T, 1)
                        pe.wait_ge(s_x1Tc, i + 1)
                        pe.wait_ge(s_qkc, i * 4)
                        for w, ps in ((wq_s, q_ps), (wk_s, k_ps)):
                            for h in range(KD):
                                for k in range(KD):
                                    last = nc.tensor.matmul(ps[:, h * UT:(h + 1) * UT], w[:, k, h * P:(h + 1) * P],
                                                            x1Ts[:, k, :], start=(k == 0), stop=(k == KD - 1))
                            last.then_inc(s_qk, 1)
                        pe.wait_ge(s_hTc, (i + 1) * 2)
                        for u in range(2):
                            for k in range(KD):
                                last = nc.tensor.matmul(v_ps[0:TT, u * D:(u + 1) * D], x1Ts[:, k, u * TT:(u + 1) * TT],
                                                        wv_s[:, k, :], start=(k == 0), stop=(k == KD - 1))
                        last.then_inc(s_v, 1)

                    patches(0, 0, 1)
                    pe.wait_ge(s_wts, 12 * 16)
                    over_units(pe, body)

                @block.scalar
                def _(act):
                    act.wait_ge(s_wTt, 1)
                    for k in range(3):
                        nc.scalar.activation(wT[:, 2 * k:2 * k + 2, :], bank[k][:].rearrange("p (k n) -> p k n", k=2),
                                             ACT.Copy).then_inc(s_wTc, 1)

                    def patches(i):
                        for k in range(3):
                            act.wait_ge(s_pT, i * KF + 2 * k + 2)
                            src = bank[k][:, 0:2 * UT].rearrange("p (k g r) -> p k g r", k=2, g=G)
                            dst = pT[:, 2 * k:2 * k + 2, :].rearrange("p k (r g) -> p k g r", g=G)
                            for h in range(2):
                                last = nc.scalar.activation(dst[:, h], src[:, h], ACT.Copy)
                            last.then_inc(s_pTc, 1)

                    def body(i, par, uses):
                        act.wait_ge(s_hT, i + 1)
                        for h in range(KD):
                            nc.scalar.activation(hTs[:, h, :], hT_ps[:, h * UT:(h + 1) * UT], ACT.Identity,
                                                 bias=colb[:, 0, h:h + 1]).then_inc(s_hTc, 1)
                        if not (isinstance(i, int) and i == NU - 1):
                            patches(i + 1)
                        act.wait_ge(s_x1T, i + 1)
                        nc.scalar.activation(x1Ts[:], x1T_ps[:, 0:2 * UT].rearrange("p (k t) -> p k t", k=2),
                                             ACT.Copy).then_inc(s_x1Tc, 1)
                        act.wait_ge(s_qkst, i * 32)
                        for n, (dst, ps, scale) in enumerate(((qs, q_ps, HD ** -0.5), (ks, k_ps, 1.0))):
                            act.wait_ge(s_qk, 2 * i + n + 1)
                            for h in range(KD):
                                nc.scalar.activation(dst[:, h, :], ps[:, h * UT:(h + 1) * UT], ACT.Identity,
                                                     bias=colb[:, n + 1, h:h + 1], scale=scale).then_inc(s_qkc, 1)

                    patches(0)
                    act.wait_ge(s_wts, 12 * 16)
                    act.wait_ge(s_bq4, 1)
                    over_units(act, body)

                @block.vector
                def _(dve):
                    dve.wait_ge(s_wts, 12 * 16)
                    nc.vector.tensor_scalar(colb[:, 1, :], colb[:, 1, :], HD ** -0.5, None, ALU.mult).then_inc(s_bq4, 1)

                    def body(i, par, uses):
                        dve.wait_ge(s_h, i + 1)
                        for u in range(2):
                            nc.vector.bn_stats(st[:, u, :], h_ps[0:TT, u * D:(u + 1) * D]).then_inc(s_hbn, 1)
                        nc.vector.tensor_tensor(hb[:, bass.ds(i * 2, 2), :], h_ps[0:TT, :].rearrange("p (u e) -> p u e", u=2),
                                                two(be_bc), ALU.add).then_inc(s_hb, 1)
                        dve.wait_ge(s_hbn, (i + 1) * 2)
                        part_waits(dve)
                        for u in range(2):
                            nc.vector.bn_aggr(mv[:, u, :], st[:, u, :]).then_inc(s_hag, 1)
                        dve.wait_ge(s_hag, (i + 1) * 2)
                        nc.vector.tensor_scalar(ve[:], mv[:, :, 1], LN_EPS, None, ALU.add).then_inc(s_hve, 1)
                        dve.wait_ge(s_hrs, i + 1)
                        dve.wait_ge(s_x1b, i)
                        for u in range(2):
                            last = nc.vector.tensor_scalar(x1s[:, u, :], h_ps[0:TT, u * D:(u + 1) * D], mv[:, u, 0:1],
                                                           rs[:, u:u + 1], ALU.subtract, ALU.mult)
                        last.then_inc(s_x1, 1)
                        dve.wait_ge(s_v, i + 1)
                        dve.wait_ge(s_vst, i * 16)
                        nc.vector.tensor_tensor(vs[:], v_ps[0:TT, :].rearrange("p (u e) -> p u e", u=2), two(bv_bc),
                                                ALU.add).then_inc(s_vc, 1)
                    over_units(dve, body)

        s_q_in = [sem("qkv_in0"), sem("qkv_in1")]
        s_z = sem("attn_zeroed")
        s_Qc, s_Kc, s_Kbd = sem("Q_ordered"), sem("K_ordered"), sem("K_blocked")
        s_ST, s_STc, s_MX, s_red = sem("ST_done"), sem("ST_copied"), sem("MX_done"), sem("max_done")
        s_mT, s_mTc, s_sub, s_exp = sem("mT_done"), sem("mT_copied"), sem("max_subtracted"), sem("exp_done")
        s_sum, s_PV, s_rec, s_ctx = sem("sum_done"), sem("PV_done"), sem("rec_done"), sem("ctx_done")
        s_cst = [sem("ctx_stored0"), sem("ctx_stored1")]

        with ExitStack() as ctx:
            qst = [sb(ctx, f"qst{k}", [96, HEADS, 2 * N]) for k in range(2)]
            kst = [sb(ctx, f"kst{k}", [96, HEADS, 2 * N]) for k in range(2)]
            vbd = [sb(ctx, f"vbd{k}", [TT, 2 * HEADS, 96]) for k in range(2)]
            Qc = [sb(ctx, f"Qc{k}", [96, 2, HEADS * N]) for k in range(2)]
            Kc = sb(ctx, "Kc", [96, 2, HEADS * N])
            Kbd = [sb(ctx, f"Kbd{k}", [96, 2 * HEADS, TT]) for k in range(2)]
            STs = [sb(ctx, f"STs{k}", [TT, IC]) for k in range(2)]
            mx = [sb(ctx, f"mx{k}", [96, 3, 3]) for k in range(2)]
            mTs = [sb(ctx, f"mTs{k}", [3, IC]) for k in range(2)]
            pTs = [sb(ctx, f"probs{k}", [TT, IC]) for k in range(2)]
            rec = sb(ctx, "rec", [96, IC])
            ctxs = [sb(ctx, f"ctxs{k}", [96, HEADS, 2 * N]) for k in range(2)]
            ST, MX, SM, PV = bank[0:2], bank[2:4], bank[4:6], bank[6:8]
            IPU = 4

            with nc.Block() as block:
                @block.sync
                def _(sp):
                    def load(i, par):
                        for a in range(3):
                            t0 = i * UT + a * 2 * N
                            sp.dma_start(qst[par][32 * a:32 * a + HD], q_view[:, :, bass.ds(t0, 2 * N)]).then_inc(s_q_in[par], 16)
                            sp.dma_start(kst[par][32 * a:32 * a + HD], k_view[:, :, bass.ds(t0, 2 * N)]).then_inc(s_q_in[par], 16)
                            src = v_flat[bass.ds(t0 * D, 2 * N * D)].rearrange("(g k d) -> k g d", k=N, d=HD)
                            sp.dma_start(vbd[par][N * a:N * a + N, :, 32 * a:32 * a + HD], src).then_inc(s_q_in[par], 16)

                    sp.wait_ge(s_z, 6)
                    load(0, 0)
                    load(1, 1)

                    def body(i, par, uses):
                        sp.wait_ge(s_PV, (i + 1) * IPU)
                        if not (isinstance(i, int) and i >= NU - 2):
                            load(i + 2, par)
                        sp.wait_ge(s_ctx, (i + 1) * IPU)
                        for a in range(3):
                            sp.dma_start(c_view[:, :, bass.ds(i * UT + a * 2 * N, 2 * N)],
                                         ctxs[par][32 * a:32 * a + HD]).then_inc(s_cst[par], 16)
                    over_units(sp, body)
                    sp.wait_ge(s_cst[0], (NU + 1) // 2 * 48)
                    sp.wait_ge(s_cst[1], NU // 2 * 48)

                @block.gpsimd
                def _(pool):
                    for k in range(2):
                        nc.gpsimd.memset(Kbd[k][:], 0.0).then_inc(s_z, 1)
                        nc.gpsimd.memset(vbd[k][:], 0.0).then_inc(s_z, 1)
                        nc.gpsimd.memset(qst[k][:], 0.0)
                        nc.gpsimd.memset(kst[k][:], 0.0).then_inc(s_z, 1)
                    pool.wait_ge(s_z, 6)

                    def body(i, par, uses):
                        pool.wait_ge(s_Kc, i + 1)
                        if not (isinstance(i, int) and i < 2):
                            pool.wait_ge(s_ST, (i - 1) * IPU)
                        part_waits(pool)
                        for a in range(3):
                            src = Kc[32 * a:32 * a + 32].rearrange("p b (g k) -> p (b g) k", k=N)
                            nc.gpsimd.tensor_copy(Kbd[par][32 * a:32 * a + 32, :, N * a:N * a + N], src).then_inc(s_Kbd, 1)
                    over_units(pool, body)

                @block.vector
                def _(dve):
                    def order(i, par, uses):
                        dve.wait_ge(s_q_in[par], uses * 9 * 16)
                        if not (isinstance(i, int) and i < 2):
                            dve.wait_ge(s_ST, (i - 1) * IPU)
                        nc.vector.tensor_copy(Qc[par][:].rearrange("p b (t j) -> p b t j", j=HEADS),
                                              qst[par][:].rearrange("p j (b t) -> p b t j", b=2)).then_inc(s_Qc, 1)
                        dve.wait_ge(s_Kbd, i * 3)
                        nc.vector.tensor_copy(Kc[:].rearrange("p b (t j) -> p b t j", j=HEADS),
                                              kst[par][:].rearrange("p j (b t) -> p b t j", b=2)).then_inc(s_Kc, 1)

                    def maxima(i, m):
                        n, b = i * IPU + m, m % 2
                        dve.wait_ge(s_MX, n + 1)
                        nc.vector.tensor_reduce(mx[b][:], MX[b][0:96, 0:3 * TT].rearrange("p (c a k) -> p c a k", c=3, a=3),
                                                AX, ALU.max).then_inc(s_red, 1)

                    def context(i, m, par, uses):
                        n, b = i * IPU + m, m % 2
                        dve.wait_ge(s_sum, n + 1)
                        dve.wait_ge(s_ctx, n)
                        nc.vector.reciprocal(rec[:], SM[b][0:96, 0:IC]).then_inc(s_rec, 1)
                        dve.wait_ge(s_rec, n + 1)
                        dve.wait_ge(s_PV, n + 1)
                        if m == 0:
                            dve.wait_ge(s_cst[par], (uses - 1) * 48)
                        t0 = (m // 2) * N + (m % 2) * (N // 2)
                        nc.vector.tensor_tensor(ctxs[par][:, :, t0:t0 + N // 2].rearrange("p j t -> p t j"),
                                                PV[b][0:96, 0:IC].rearrange("p (t j) -> p t j", j=HEADS),
                                                rec[:].rearrange("p (t j) -> p t j", j=HEADS), ALU.mult).then_inc(s_ctx, 1)

                    def body(i, par, uses):
                        for m in range(IPU):
                            if m + 1 < IPU:
                                maxima(i, m + 1)
                            elif not (isinstance(i, int) and i == NU - 1):
                                maxima(i + 1, 0)
                            context(i, m, par, uses)
                            if m == 1 and not (isinstance(i, int) and i == NU - 1):
                                order(i + 1, 1 - par, uses + par)
                    dve.wait_ge(s_z, 6)
                    order(0, 0, 1)
                    maxima(0, 0)
                    over_units(dve, body)

                @block.scalar
                def _(act):
                    def copy_scores(i, m):
                        n, b = i * IPU + m, m % 2
                        act.wait_ge(s_ST, n + 1)
                        if not (isinstance(n, int) and n < 2):
                            act.wait_ge(s_MX, n - 1)
                        nc.scalar.activation(STs[b][:], ST[b][0:TT, 0:IC], ACT.Copy).then_inc(s_STc, 1)

                    def neg_max(i, m):
                        n, b = i * IPU + m, m % 2
                        act.wait_ge(s_mT, n + 1)
                        if not (isinstance(n, int) and n < 2):
                            act.wait_ge(s_sub, n - 1)
                        nc.scalar.activation(mTs[b][:], SM[b][0:3, 0:IC], ACT.Copy, scale=-1.0).then_inc(s_mTc, 1)

                    def exponent(i, m):
                        n, b = i * IPU + m, m % 2
                        act.wait_ge(s_sub, n + 1)
                        if not (isinstance(n, int) and n < 2):
                            act.wait_ge(s_PV, n - 1)
                        nc.scalar.activation(pTs[b][:], ST[b][0:TT, 0:IC], ACT.Exp).then_inc(s_exp, 1)

                    def body(i, par, uses):
                        for m in range(IPU):
                            nxt = (i, m + 1) if m + 1 < IPU else (i + 1, 0)
                            if isinstance(i, int) and i == NU - 1 and m == IPU - 1:
                                nxt = None
                            if nxt:
                                copy_scores(*nxt)
                            exponent(i, m)
                            if nxt:
                                neg_max(*nxt)
                    copy_scores(0, 0)
                    neg_max(0, 0)
                    over_units(act, body)

                @block.tensor
                def _(pe):
                    def scores(i, m, par):
                        n, b = i * IPU + m, m % 2
                        if m == 0:
                            pe.wait_ge(s_Qc, i + 1)
                            pe.wait_ge(s_Kbd, (i + 1) * 3)
                        if not (isinstance(n, int) and n < 2):
                            pe.wait_ge(s_exp, n - 1)
                        for g in range(8):
                            gg = (m // 2) * HEADS + (m % 2) * 8 + g
                            o = (m % 2) * IC + g * N
                            last = nc.tensor.matmul(ST[b][0:TT, g * N:(g + 1) * N], Kbd[par][:, gg, :],
                                                    Qc[par][:, m // 2, o:o + N], start=(g == 0), stop=(g == 7),
                                                    skip_group_check=True)
                        last.then_inc(s_ST, 1)

                    def turn(i, m):
                        n, b = i * IPU + m, m % 2
                        pe.wait_ge(s_STc, n + 1)
                        if not (isinstance(n, int) and n < 2):
                            pe.wait_ge(s_red, n - 1)
                        for c in range(3):
                            last = nc.tensor.transpose(MX[b][0:96, c * TT:(c + 1) * TT], STs[b][:, c * 96:(c + 1) * 96],
                                                       ident[0:TT, 0:TT])
                        last.then_inc(s_MX, 1)

                    def turn_max(i, m):
                        n, b = i * IPU + m, m % 2
                        pe.wait_ge(s_red, n + 1)
                        if not (isinstance(n, int) and n < 2):
                            pe.wait_ge(s_rec, n - 1)
                        for c in range(3):
                            last = nc.tensor.transpose(SM[b][0:3, c * 96:(c + 1) * 96], mx[b][:, c, :], ident[0:96, 0:96])
                        last.then_inc(s_mT, 1)

                    def subtract(i, m):
                        n, b = i * IPU + m, m % 2
                        pe.wait_ge(s_mTc, n + 1)
                        nc.tensor.matmul(ST[b][0:TT, 0:IC], mk[0:3, M_IND:M_IND + TT], mTs[b][:], start=False, stop=True,
                                         skip_group_check=True).then_inc(s_sub, 1)

                    def values(i, m, par):
                        n, b = i * IPU + m, m % 2
                        pe.wait_ge(s_exp, n + 1)
                        nc.tensor.matmul(SM[b][0:96, 0:IC], mk[0:TT, M_OBD:M_OBD + 96], pTs[b][:], start=True,
                                         stop=True).then_inc(s_sum, 1)
                        if not (isinstance(n, int) and n < 2):
                            pe.wait_ge(s_ctx, n - 1)
                        for g in range(8):
                            gg = (m // 2) * HEADS + (m % 2) * 8 + g
                            last = nc.tensor.matmul(PV[b][0:96, g * N:(g + 1) * N], vbd[par][:, gg, :],
                                                    pTs[b][:, g * N:(g + 1) * N], start=(g == 0), stop=(g == 7),
                                                    skip_group_check=True)
                        last.then_inc(s_PV, 1)

                    def body(i, par, uses):
                        for m in range(IPU):
                            nxt = (i, m + 1, par) if m + 1 < IPU else (i + 1, 0, 1 - par)
                            if isinstance(i, int) and i == NU - 1 and m == IPU - 1:
                                nxt = None
                            if nxt:
                                scores(*nxt)
                            subtract(i, m)
                            if nxt:
                                turn(*nxt[:2])
                            if m == 0:
                                pe.wait_ge(s_q_in[par], uses * 9 * 16)
                            values(i, m, par)
                            if nxt:
                                turn_max(*nxt[:2])
                    pe.wait_ge(s_z, 6)
                    scores(0, 0, 0)
                    turn(0, 0)
                    turn_max(0, 0)
                    over_units(pe, body)

        s_c_in = [sem("ctx_in0"), sem("ctx_in1")]
        names = ("o_done r_done r_bn r_ag r_rs r_ve h2_ve n1_done ng_done h2_done h_bn2 h_ag2 h2_rs x2_done x2T_done x2T_copied "
                 "g_done g_max g_sub g_exp g_sum g_rec p_done X_done Bp_done gt_done eq_done eqL_done cnt_done "
                 "rank_done S_done SP_done xin_done xin_copied SPT_done SPT_copied SPT_stored").split()
        S = {n: sem(n) for n in names}
        s_w1 = [sem("w1_in0"), sem("w1_in1")]
        s_w2 = [sem("w2_in0"), sem("w2_in1")]
        s_zy = sem("xin_zeroed")
        xinT = sb(top, "xinT", [P, KD, E, PSLOTS])
        w1s = [sb(top, f"w1s{k}", [P, KD, HID]) for k in range(2)]
        w2s = [sb(top, f"w2s{k}", [P, KH, D]) for k in range(2)]

        with ExitStack() as ctx:
            cT = [sb(ctx, f"cT{k}", [P, KD, UT]) for k in range(2)]
            r = sb(ctx, "r", [TT, 2, D])
            x2 = sb(ctx, "x2", [TT, 2, D])
            x2T = sb(ctx, "x2T", [P, KD, UT])
            st = sb(ctx, "st2", [TT, 2, 6])
            mv = sb(ctx, "mv2", [TT, 2, 2])
            rs = sb(ctx, "rs2", [TT, 2])
            ve = sb(ctx, "ve2", [TT, 2])
            gm = sb(ctx, "gm", [TT, 2])
            gs = sb(ctx, "gs", [TT, 2])
            gr = sb(ctx, "gr", [TT, 2])
            ge = sb(ctx, "ge", [TT, 2, E])
            pr = sb(ctx, "pr", [TT, 2, E])
            X = sb(ctx, "X", [TT, 2, E, N])
            gt = sb(ctx, "gt", [TT, 2, E, N])
            eq = sb(ctx, "eq", [TT, 2, E, N])
            rank = sb(ctx, "rank", [TT, 2, E])
            Sm = sb(ctx, "Sm", [TT, 2, E, TS])
            SP = sb(ctx, "SP", [TT, 2, E, TS])
            SPTs = sb(ctx, "SPTs", [TT, 2, 2 * TT])
            o_ps, x2T_ps, g_ps, B_ps, xin_ps, spt_ps = bank[0], bank[1], bank[2], bank[3:5], bank[5:7], bank[7]

            with nc.Block() as block:
                def halves(ap):
                    return ap.rearrange("p (u e) -> p u e", u=2)

                @block.sync
                def _(sp):
                    cload = cT_d.rearrange("(h p) t -> p h t", p=P)

                    def load(i, par):
                        sp.dma_start(cT[par][:], cload[:, :, bass.ds(i * UT, UT)]).then_inc(s_c_in[par], 16)
                    load(0, 0)
                    load(1, 1)
                    for e in range(2):
                        sp.dma_start(w1s[e][:], w1[e].rearrange("(k p) n -> p k n", p=P)).then_inc(s_w1[e], 16)
                        sp.dma_start(w2s[e][:], w2[e].rearrange("(k p) n -> p k n", p=P)).then_inc(s_w2[e], 16)

                    def body(i, par, uses):
                        sp.wait_ge(S["o_done"], i + 1)
                        if not (isinstance(i, int) and i >= NU - 2):
                            load(i + 2, par)
                        sp.wait_ge(S["SPT_copied"], (i + 1))
                        sp.dma_start(spt_d[bass.ds(i * 2, 2)].rearrange("u p n -> p u n"), SPTs[:]).then_inc(S["SPT_stored"], 16)
                    over_units(sp, body)
                    sp.wait_ge(S["SPT_stored"], NU * 16)

                @block.gpsimd
                def _(pool):
                    def body(i, par, uses):
                        pool.wait_ge(S["r_ve"], i + 1)
                        nc.gpsimd.tensor_tensor(rs[:], ve[:], nh[:], ALU.pow).then_inc(S["r_rs"], 1)
                        pool.wait_ge(S["n1_done"], i + 1)
                        nc.gpsimd.tensor_tensor(r[:], r[:], two(ga_bc), ALU.mult).then_inc(S["ng_done"], 1)
                        pool.wait_ge(S["h2_ve"], i + 1)
                        nc.gpsimd.tensor_tensor(rs[:], ve[:], nh[:], ALU.pow).then_inc(S["h2_rs"], 1)
                        pool.wait_ge(S["p_done"], i + 1)
                        pool.wait_ge(S["Bp_done"], i * 2)
                        i36 = mk[0:TT, M_I36:M_I36 + N].unsqueeze(1).to_broadcast([TT, E, N])
                        for u in range(2):
                            nc.gpsimd.tensor_tensor(X[:, u], pr[:, u, :].unsqueeze(2).to_broadcast([TT, E, N]), i36,
                                                    ALU.mult).then_inc(S["X_done"], 1)
                        low = mk[0:TT, M_LOW:M_LOW + N].unsqueeze(1).to_broadcast([TT, E, N])
                        for u in range(2):
                            pool.wait_ge(S["eq_done"], i * 2 + u + 1)
                            nc.gpsimd.tensor_tensor(eq[:, u], eq[:, u], low, ALU.mult).then_inc(S["eqL_done"], 1)
                    over_units(pool, body)

                @block.vector
                def _(dve):
                    def norm(i, src, dst, keys):
                        bn, ag, rsq, done = keys
                        for u in range(2):
                            nc.vector.bn_stats(st[:, u, :], src[:, u, :]).then_inc(S[bn], 1)
                        dve.wait_ge(S[bn], (i + 1) * 2)
                        part_waits(dve)
                        for u in range(2):
                            nc.vector.bn_aggr(mv[:, u, :], st[:, u, :]).then_inc(S[ag], 1)
                        dve.wait_ge(S[ag], (i + 1) * 2)
                        nc.vector.tensor_scalar(ve[:], mv[:, :, 1], LN_EPS, None, ALU.add).then_inc(S[rsq[:-2] + "ve"], 1)
                        dve.wait_ge(S[rsq], i + 1)
                        for u in range(2):
                            last = nc.vector.tensor_scalar(dst[:, u, :], src[:, u, :], mv[:, u, 0:1], rs[:, u:u + 1],
                                                           ALU.subtract, ALU.mult)
                        last.then_inc(S[done], 1)

                    nc.vector.memset(xinT[:, :, :, SLOTS:PSLOTS], 0.0).then_inc(s_zy, 1)

                    def body(i, par, uses):
                        pair = bass.ds(i * 2, 2)
                        dve.wait_ge(S["o_done"], i + 1)
                        nc.vector.tensor_tensor(r[:], halves(o_ps[0:TT, :]), x1b[:, pair, :], ALU.add).then_inc(S["r_done"], 1)
                        dve.wait_ge(S["r_done"], i + 1)
                        norm(i, r, r, ("r_bn", "r_ag", "r_rs", "n1_done"))
                        dve.wait_ge(S["ng_done"], i + 1)
                        nc.vector.tensor_tensor(hb[:, pair, :], r[:], hb[:, pair, :], ALU.add).then_inc(S["h2_done"], 1)
                        dve.wait_ge(S["h2_done"], i + 1)
                        part_waits(dve)
                        norm(i, hb[:, pair, :], x2, ("h_bn2", "h_ag2", "h2_rs", "x2_done"))
                        dve.wait_ge(S["g_done"], i + 1)
                        gps = g_ps[0:TT, 0:2 * E].rearrange("p (u e) -> p u e", u=2)
                        nc.vector.tensor_reduce(gm[:], gps, AX, ALU.max).then_inc(S["g_max"], 1)
                        dve.wait_ge(S["g_max"], i + 1)
                        nc.vector.tensor_tensor(ge[:], gps, gm[:].unsqueeze(2).to_broadcast([TT, 2, E]),
                                                ALU.subtract).then_inc(S["g_sub"], 1)
                        dve.wait_ge(S["g_exp"], i + 1)
                        nc.vector.tensor_reduce(gs[:], ge[:], AX, ALU.add).then_inc(S["g_sum"], 1)
                        dve.wait_ge(S["g_sum"], i + 1)
                        nc.vector.reciprocal(gr[:], gs[:]).then_inc(S["g_rec"], 1)
                        dve.wait_ge(S["g_rec"], i + 1)
                        nc.vector.tensor_tensor(pr[:], ge[:], gr[:].unsqueeze(2).to_broadcast([TT, 2, E]),
                                                ALU.mult).then_inc(S["p_done"], 1)
                        dve.wait_ge(S["p_done"], i + 1)
                        for u in range(2):
                            dve.wait_ge(S["Bp_done"], i * 2 + u + 1)
                            bp = B_ps[u][0:TT, 0:E * N].rearrange("p (e t) -> p e t", e=E)
                            own = pr[:, u, :].unsqueeze(2).to_broadcast([TT, E, N])
                            nc.vector.tensor_tensor(eq[:, u], bp, own, ALU.is_equal).then_inc(S["eq_done"], 1)
                            nc.vector.tensor_tensor(gt[:, u], bp, own, ALU.is_gt).then_inc(S["gt_done"], 1)
                        for u in range(2):
                            dve.wait_ge(S["gt_done"], i * 2 + u + 1)
                            dve.wait_ge(S["eqL_done"], i * 2 + u + 1)
                            nc.vector.tensor_tensor(gt[:, u], gt[:, u], eq[:, u], ALU.add).then_inc(S["cnt_done"], 1)
                        for u in range(2):
                            dve.wait_ge(S["cnt_done"], i * 2 + u + 1)
                            nc.vector.tensor_reduce(rank[:, u, :], gt[:, u], AX, ALU.add).then_inc(S["rank_done"], 1)
                        iota = mk[0:TT, M_IOTA:M_IOTA + TS].unsqueeze(1).to_broadcast([TT, E, TS])
                        for u in range(2):
                            dve.wait_ge(S["rank_done"], i * 2 + u + 1)
                            nc.vector.tensor_tensor(Sm[:, u], rank[:, u, :].unsqueeze(2).to_broadcast([TT, E, TS]), iota,
                                                    ALU.is_equal).then_inc(S["S_done"], 1)
                        for u in range(2):
                            dve.wait_ge(S["S_done"], i * 2 + u + 1)
                            nc.vector.tensor_tensor(SP[:, u], Sm[:, u], pr[:, u, :].unsqueeze(2).to_broadcast([TT, E, TS]),
                                                    ALU.mult).then_inc(S["SP_done"], 1)
                        dve.wait_ge(s_zy, 1)
                        for u in range(2):
                            dve.wait_ge(S["xin_done"], i * 2 + u + 1)
                            for h in range(KD):
                                last = nc.vector.tensor_copy(xinT[:, h, :, bass.ds((i * 2 + u) * TS, TS)],
                                                             xin_ps[u][:, h * E * TS:(h + 1) * E * TS].rearrange("p (e s) -> p e s", e=E))
                            last.then_inc(S["xin_copied"], 1)
                    over_units(dve, body)

                @block.scalar
                def _(act):
                    def body(i, par, uses):
                        act.wait_ge(S["x2T_done"], i + 1)
                        nc.scalar.activation(x2T[:], x2T_ps[:, 0:2 * UT].rearrange("p (k t) -> p k t", k=2),
                                             ACT.Copy).then_inc(S["x2T_copied"], 1)
                        act.wait_ge(S["g_sub"], i + 1)
                        nc.scalar.activation(ge[:], ge[:], ACT.Exp).then_inc(S["g_exp"], 1)
                        act.wait_ge(S["SPT_done"], i + 1)
                        act.wait_ge(S["SPT_stored"], i * 16)
                        nc.scalar.activation(SPTs[:], spt_ps[0:TT, 0:4 * TT].rearrange("p (u n) -> p u n", u=2),
                                             ACT.Copy).then_inc(S["SPT_copied"], 1)
                    over_units(act, body)

                @block.tensor
                def _(pe):
                    def body(i, par, uses):
                        pe.wait_ge(s_c_in[par], uses * 16)
                        pe.wait_ge(S["r_done"], i)
                        for u in range(2):
                            for k in range(KD):
                                last = nc.tensor.matmul(o_ps[0:TT, u * D:(u + 1) * D], cT[par][:, k, u * TT:(u + 1) * TT],
                                                        wo_s[:, k, :], start=(k == 0), stop=(k == KD - 1))
                        last.then_inc(S["o_done"], 1)
                        pe.wait_ge(S["x2_done"], i + 1)
                        for h in range(KD):
                            for u in range(2):
                                last = nc.tensor.transpose(x2T_ps[:, h * UT + u * TT:h * UT + (u + 1) * TT],
                                                           x2[:, u, h * P:(h + 1) * P], ident[0:TT, 0:TT])
                        last.then_inc(S["x2T_done"], 1)
                        pe.wait_ge(S["x2T_copied"], i + 1)
                        for u in range(2):
                            for k in range(KD):
                                last = nc.tensor.matmul(g_ps[0:TT, u * E:(u + 1) * E], x2T[:, k, u * TT:(u + 1) * TT],
                                                        gate_s[:, k, :], start=(k == 0), stop=(k == KD - 1))
                        last.then_inc(S["g_done"], 1)
                        for u in range(2):
                            pe.wait_ge(S["X_done"], i * 2 + u + 1)
                            nc.tensor.matmul(B_ps[u][0:TT, 0:E * N], mk[0:TT, M_BLK:M_BLK + TT],
                                             X[:, u].rearrange("p e t -> p (e t)"), start=True, stop=True).then_inc(S["Bp_done"], 1)
                        for u in range(2):
                            pe.wait_ge(S["S_done"], i * 2 + u + 1)
                            pe.wait_ge(S["xin_copied"], i * 2)
                            for h in range(KD):
                                last = nc.tensor.matmul(xin_ps[u][:, h * E * TS:(h + 1) * E * TS], x2[:, u, h * P:(h + 1) * P],
                                                        Sm[:, u].rearrange("p e s -> p (e s)"), start=True, stop=True)
                            last.then_inc(S["xin_done"], 1)
                        pe.wait_ge(S["SP_done"], i * 2 + 2)
                        for u in range(2):
                            for q in range(2):
                                last = nc.tensor.transpose(spt_ps[0:TT, (2 * u + q) * TT:(2 * u + q + 1) * TT],
                                                           SP[:, u, 4 * q:4 * q + 4, :].rearrange("p e s -> p (e s)"),
                                                           ident[0:TT, 0:TT])
                        last.then_inc(S["SPT_done"], 1)
                    over_units(pe, body)

        s_l1, s_gelu, s_y, s_yc = sem("l1_done"), sem("gelu_done"), sem("y_done"), sem("y_copied")
        HS = SLOTS // 2
        with ExitStack() as ctx:
            hT = sb(ctx, "hT", [P, KH, SLOTS])
            with nc.Block() as block:
                def experts(eng, body):
                    body(0, 0, 1)
                    with eng.Fori(0, (E - 2) // 2) as p:
                        body(p * 2 + 1, 1, p + 1)
                        body(p * 2 + 2, 0, p + 2)
                    body(E - 1, 1, E // 2)

                @block.sync
                def _(sp):
                    def load(e, par):
                        sp.wait_ge(s_l1, e * 16 - 16)
                        sp.dma_start(w1s[par][:], w1[bass.ds(e, 1)].rearrange("o (k p) n -> p (o k) n", p=P)).then_inc(s_w1[par], 16)
                        sp.wait_ge(s_y, e * 4 - 4)
                        sp.dma_start(w2s[par][:], w2[bass.ds(e, 1)].rearrange("o (k p) n -> p (o k) n", p=P)).then_inc(s_w2[par], 16)
                    with sp.Fori(1, E // 2) as p:
                        load(p * 2, 0)
                        load(p * 2 + 1, 1)

                @block.tensor
                def _(pe):
                    def body(e, par, uses):
                        pe.wait_ge(s_w1[par], uses * 16)
                        for m in range(KH):
                            for n in range(2):
                                j = (2 * m + n) % 4
                                if not (isinstance(e, int) and e == 0 and 2 * m + n < 4):
                                    pe.wait_ge(s_gelu, e * 16 + 2 * m + n - 3)
                                for k in range(KD):
                                    last = nc.tensor.matmul(bank[j][:, 0:HS], w1s[par][:, k, m * P:(m + 1) * P],
                                                            xinT[:, k, e, n * HS:(n + 1) * HS] if isinstance(e, int) else
                                                            xinT[:, k, bass.ds(e, 1), n * HS:(n + 1) * HS],
                                                            start=(k == 0), stop=(k == KD - 1))
                                last.then_inc(s_l1, 1)
                        pe.wait_ge(s_w2[par], uses * 16)
                        pe.wait_ge(s_gelu, (e + 1) * 16)
                        for f in range(KD):
                            for n in range(2):
                                pe.wait_ge(s_yc, e * 4)
                                for m in range(KH):
                                    last = nc.tensor.matmul(bank[4 + 2 * f + n][:, 0:HS], w2s[par][:, m, f * P:(f + 1) * P],
                                                            hT[:, m, n * HS:(n + 1) * HS], start=(m == 0), stop=(m == KH - 1))
                                last.then_inc(s_y, 1)
                    experts(pe, body)

                @block.scalar
                def _(act):
                    def body(e, par, uses):
                        act.wait_ge(s_y, e * 4)
                        for m in range(KH):
                            for n in range(2):
                                act.wait_ge(s_l1, e * 16 + 2 * m + n + 1)
                                nc.scalar.activation(hT[:, m, n * HS:(n + 1) * HS], bank[(2 * m + n) % 4][:, 0:HS],
                                                     ACT.Gelu).then_inc(s_gelu, 1)
                    experts(act, body)

                @block.vector
                def _(dve):
                    def body(e, par, uses):
                        for f in range(KD):
                            for n in range(2):
                                dve.wait_ge(s_y, e * 4 + 2 * f + n + 1)
                                nc.vector.tensor_copy(xinT[:, f, bass.ds(e, 1), n * HS:(n + 1) * HS],
                                                      bank[4 + 2 * f + n][:, 0:HS].unsqueeze(1)).then_inc(s_yc, 1)
                    experts(dve, body)

        s_spt = [sem("spt_in0"), sem("spt_in1")]
        s_ys, s_yt, s_ysl, s_comb, s_out = sem("y_gathered"), sem("y_turned"), sem("y_slots"), sem("combined"), sem("summed")
        s_ost = [sem("out_stored0"), sem("out_stored1")]
        with ExitStack() as ctx:
            spt = [sb(ctx, f"spt{k}", [TT, 2, 2 * TT]) for k in range(2)]
            ys = [sb(ctx, f"ys{k}", [P, 2, KD, E, TS]) for k in range(2)]
            ysl = [sb(ctx, f"ysl{k}", [TT, 2, 2, D]) for k in range(2)]
            os_ = [sb(ctx, f"os{k}", [TT, 2, D]) for k in range(2)]
            YT, CB = (bank[0:2], bank[2:4]), bank[4:6]
            with nc.Block() as block:
                @block.sync
                def _(sp):
                    def load(i, par):
                        sp.dma_start(spt[par][:], spt_d[bass.ds(i * 2, 2)].rearrange("u p n -> p u n")).then_inc(s_spt[par], 16)
                    load(0, 0)
                    load(1, 1)
                    rows = out.rearrange("b n e -> (b n) e")

                    def body(i, par, uses):
                        sp.wait_ge(s_comb, i + 1)
                        if not (isinstance(i, int) and i >= NU - 2):
                            load(i + 2, par)
                        sp.wait_ge(s_out, i + 1)
                        if isinstance(i, int) and i == NU - 1:
                            t0 = i * UT
                            sp.dma_start(rows[t0:t0 + TT, :], os_[par][:, 0, :]).then_inc(s_ost[par], 16)
                            left = B * N - t0 - TT
                            sp.dma_start(rows[t0 + TT:t0 + TT + left, :], os_[par][0:left, 1, :]).then_inc(s_ost[par], 16)
                        else:
                            sp.dma_start(rows[bass.ds(i * UT, UT), :].rearrange("(u t) e -> t u e", u=2), os_[par][:]).then_inc(s_ost[par], 16)
                    over_units(sp, body)
                    sp.wait_ge(s_ost[0], (NU + 1) // 2 * 16 + 16)
                    sp.wait_ge(s_ost[1], NU // 2 * 16)

                @block.gpsimd
                def _(pool):
                    def body(i, par, uses):
                        if not (isinstance(i, int) and i < 2):
                            pool.wait_ge(s_yt, i - 1)
                        for u in range(2):
                            for f in range(KD):
                                last = nc.gpsimd.tensor_copy(ys[par][:, u, f], xinT[:, f, :, bass.ds((i * 2 + u) * TS, TS)])
                        last.then_inc(s_ys, 1)
                    over_units(pool, body)

                @block.tensor
                def _(pe):
                    def turn(i, par):
                        pe.wait_ge(s_ys, i + 1)
                        if not (isinstance(i, int) and i < 2):
                            pe.wait_ge(s_ysl, (i - 1) * 2)
                        for u in range(2):
                            for q in range(2):
                                for f in range(KD):
                                    last = nc.tensor.transpose(YT[par][u][0:TT, q * D + f * P:q * D + (f + 1) * P],
                                                               ys[par][:, u, f, 4 * q:4 * q + 4, :].rearrange("p e s -> p (e s)"), ident)
                        last.then_inc(s_yt, 1)

                    def body(i, par, uses):
                        if not (isinstance(i, int) and i == NU - 1):
                            turn(i + 1, 1 - par)
                        pe.wait_ge(s_ysl, (i + 1) * 2)
                        pe.wait_ge(s_spt[par], uses * 16)
                        if not (isinstance(i, int) and i < 2):
                            pe.wait_ge(s_out, i - 1)
                        for u in range(2):
                            for q in range(2):
                                last = nc.tensor.matmul(CB[par][0:TT, u * D:(u + 1) * D], spt[par][:, u, q * TT:(q + 1) * TT],
                                                        ysl[par][:, u, q, :], start=(q == 0), stop=(q == 1))
                        last.then_inc(s_comb, 1)
                    turn(0, 0)
                    over_units(pe, body)

                @block.scalar
                def _(act):
                    def body(i, par, uses):
                        act.wait_ge(s_yt, i + 1)
                        if not (isinstance(i, int) and i < 2):
                            act.wait_ge(s_comb, i - 1)
                        for u in range(2):
                            nc.scalar.activation(ysl[par][:, u], YT[par][u][0:TT, :].rearrange("p (q e) -> p q e", q=2),
                                                 ACT.Copy).then_inc(s_ysl, 1)
                    over_units(act, body)

                @block.vector
                def _(dve):
                    def body(i, par, uses):
                        dve.wait_ge(s_comb, i + 1)
                        dve.wait_ge(s_ost[par], (uses - 1) * 16)
                        nc.vector.tensor_tensor(os_[par][:], CB[par][0:TT, :].rearrange("p (u e) -> p u e", u=2),
                                                hb[:, bass.ds(i * 2, 2), :], ALU.add).then_inc(s_out, 1)
                    over_units(dve, body)


_INS = ['x', 'L0_tok_W', 'L0_tok_b', 'L0_attn_wq', 'L0_attn_bq', 'L0_attn_wk', 'L0_attn_bk', 'L0_attn_wv', 'L0_attn_bv',
        'L0_attn_wo', 'L0_attn_bo', 'L0_attn_gamma', 'L0_attn_beta', 'L0_ffn_gate_w', 'L0_ffn_w1', 'L0_ffn_w2']


def kernel(**inputs):
    import concourse.bacc as _bacc
    from concourse.bass_utils import run_bass_kernel_spmd as _run

    nc = _bacc.Bacc("TRN2", target_bir_lowering=False, num_devices=1)
    arrays, args = {}, []
    for name in _INS:
        a = np.ascontiguousarray(inputs[name])
        arrays[f"in_{name}"] = a
        args.append(nc.dram_tensor(f"in_{name}", a.shape, mybir.dt.from_np(a.dtype), kind="ExternalInput").ap())
    arrays["in_masks"] = shape_masks()
    args.append(nc.dram_tensor("in_masks", arrays["in_masks"].shape, F32, kind="ExternalInput").ap())
    args.append(nc.dram_tensor("out_0", (B, N, D), F32, kind="ExternalOutput").ap())
    build(nc, *args)
    r = _run(nc, [arrays], core_ids=[0])
    return r.results[0]["out_0"]
```

```python
from contextlib import ExitStack

import numpy as np

import concourse.bass as bass
from concourse import mybir

F32 = mybir.dt.float32
F32R = mybir.dt.float32r
ALU = mybir.AluOpType
ACT = mybir.ActivationFunctionType
AX = mybir.AxisListType.X

P = 128
B, C, IMG, PATCH = 64, 3, 96, 16
G = IMG // PATCH
N = G * G
D = 256
KD = D // P
KF = C * PATCH * PATCH // P
HEADS, HD = 16, 16
E, CAP = 8, 2 * N // 8
HID = 1024
KH = HID // P
UB = 6
UT = UB * N
NU = -(-B // UB)
LASTB = B - (NU - 1) * UB
TT = 3 * N
T = NU * UT
SLOTS = B * CAP
PSLOTS = NU * UB * CAP
TS = 3 * CAP
LN_EPS = 1e-5

M_ID = 0
M_BLK = M_ID + P
M_I36 = M_BLK + TT
M_LOW = M_I36 + N
M_IOTA = M_LOW + N
M_M8 = M_IOTA + TS
M_A3 = M_M8 + 8
M_END = M_A3 + 3
AB = 8
AU = B // AB
AI = HEADS // 2
CST = 2 * AB * 16


def shape_masks():
    m = np.zeros((P, M_END), np.float32)
    t = np.arange(TT)
    m[:, M_ID:M_ID + P] = np.eye(P)
    m[:TT, M_BLK:M_BLK + TT] = (t[:, None] // N) == (t[None, :] // N)
    m[:TT, M_I36:M_I36 + N] = (t[:, None] % N) == np.arange(N)[None, :]
    m[:TT, M_LOW:M_LOW + N] = np.arange(N)[None, :] < (t[:, None] % N)
    s = np.arange(TS)
    m[:TT, M_IOTA:M_IOTA + TS] = np.where(s[None, :] // CAP == t[:, None] // N, s[None, :] % CAP, -1)
    m[:, M_M8:M_M8 + AB] = np.arange(P)[:, None] // HD == np.arange(AB)[None, :]
    m[:TT, M_A3:M_A3 + 3] = (t[:, None] // N) == np.arange(3)[None, :]
    return m


def over_units(eng, body, units=NU):
    for i in range(2):
        body(i, i, 1)
    pairs = (units - 4) // 2
    with eng.Fori(0, pairs) as p:
        body(p * 2 + 2, 0, p + 2)
        body(p * 2 + 3, 1, p + 2)
    for i in range(2 * pairs + 2, units):
        body(i, i % 2, i // 2 + 1)


def last_unit(i):
    return isinstance(i, int) and i == NU - 1


def build(nc, x, tok_w, tok_b, wq, bq, wk, bk, wv, bv, wo, bo, gamma, beta, gate_w, w1, w2, masks, out):
    def dram(name, shape):
        return nc.dram_tensor(name, shape, F32).ap()

    qT_d = dram("qT_scratch", [D, T])
    kT_d = dram("kT_scratch", [D, T])
    v_d = dram("v_scratch", [T, D])
    c_d = dram("c_scratch", [T, D])
    spt_d = dram("spt_scratch", [NU * 2, TT, 2 * TT])
    q_view = qT_d.rearrange("(j d) t -> d j t", d=HD)
    k_view = kT_d.rearrange("(j d) t -> d j t", d=HD)
    c_view = c_d[0:B * N, :].rearrange("(b n) e -> b (n e)", b=B).rearrange("b (m h q d) -> b m h q d", h=2, q=N, d=HD)
    v_flat = v_d.rearrange("t e -> (t e)")

    top = ExitStack()
    with top:
        def sem(name):
            return top.enter_context(nc.semaphore(name))

        def sb(ctx, name, shape):
            return ctx.enter_context(nc.sbuf_tensor(name, shape, F32))

        def psum(ctx, name):
            return ctx.enter_context(nc.psum_tensor(name, [P, 512], F32))

        bank = [psum(top, f"bank{i}") for i in range(8)]
        mk = sb(top, "mk", [P, M_END])
        ident = mk[:, M_ID:M_ID + P]
        colb = sb(top, "colb", [P, 3, KD])
        rowb = sb(top, "rowb", [TT, 4, D])
        wo_s = sb(top, "wo_s", [P, KD, D])
        gate_s = sb(top, "gate_s", [P, KD, E])
        nh = sb(top, "nh", [TT, 2])
        hb = sb(top, "hb", [TT, 2 * NU, D])
        x1b = sb(top, "x1b", [TT, 2 * NU, D])
        s_const = sem("const_in")

        s_parted = sem("waits_parted")

        def part_waits(eng):
            eng.sem_inc(s_parted, 1)

        bv_bc, bo_bc, ga_bc, be_bc = (rowb[:, k, :] for k in range(4))

        def two(ap):
            return ap.unsqueeze(1).to_broadcast([TT, 2, D])

        s_wts = sem("weights_in")
        s_x = [sem("x_in0"), sem("x_in1")]
        s_wTt, s_wTc = sem("wT_transposed"), sem("wT_copied")
        s_hve = sem("h_var_eps")
        s_nh = sem("minus_half")
        s_xr = sem("pixels_regrouped")
        s_pT, s_pTc = sem("patches_transposed"), sem("patches_copied")
        s_hT, s_hTc = sem("hT_done"), sem("hT_copied")
        s_h, s_hbn, s_hag, s_hrs, s_x1, s_hb = (sem(n) for n in ("h_done", "h_bn", "h_aggr", "h_rstd", "x1_done", "hb_done"))
        s_x1b = sem("x1b_done")
        s_x1T, s_x1Tc = sem("x1T_done"), sem("x1T_copied")
        s_qk, s_qkc, s_v, s_vc = sem("qk_done"), sem("qk_copied"), sem("v_done"), sem("v_copied")
        s_qkst, s_vst = sem("qk_stored"), sem("v_stored")
        s_bq4 = sem("bq_scaled")

        with ExitStack() as ctx, nc.allow_non_contiguous_dma(reason="bias columns"):
            xraw = [sb(ctx, f"xraw{k}", [UB * G, C, PATCH * IMG]) for k in range(2)]
            xr = sb(ctx, "xr", [UB * G, C, G, PATCH * PATCH])
            wnat = sb(ctx, "wnat", [P, KD, C * PATCH * PATCH])
            wT = sb(ctx, "wT", [P, KF, D])
            wq_s, wk_s, wv_s = (sb(ctx, n, [P, KD, D]) for n in ("wq_s", "wk_s", "wv_s"))
            pT = sb(ctx, "pT", [P, KF, UT])
            hTs = sb(ctx, "hTs", [P, KD, UT])
            x1s = sb(ctx, "x1s", [TT, 2, D])
            x1Ts = sb(ctx, "x1Ts", [P, KD, UT])
            qs = sb(ctx, "qs", [P, KD, UT])
            ks = sb(ctx, "ks", [P, KD, UT])
            vs = sb(ctx, "vs", [TT, 2, D])
            st = sb(ctx, "st", [TT, 2, 6])
            mv = sb(ctx, "mv", [TT, 2, 2])
            rs = sb(ctx, "rs", [TT, 2])
            ve = sb(ctx, "ve", [TT, 2])
            hT_ps, h_ps, x1T_ps, q_ps, k_ps, v_ps = bank[3], bank[4], bank[5], bank[6], bank[7], bank[5]

            with nc.Block() as block:
                @block.sync
                def _(sp):
                    def load_x(i, par):
                        nb = LASTB if isinstance(i, int) and i == NU - 1 else UB
                        for c in range(C):
                            src = x[bass.ds(i * UB, nb), c, :, :].rearrange("b (g r) w -> b g (r w)", g=G)
                            sp.dma_start(xraw[par][0:nb * G, c, :], src).then_inc(s_x[par], 16)

                    load_x(0, 0)
                    sp.dma_start(mk[:], masks).then_inc(s_const, 16)
                    sp.dma_start(wnat[:], tok_w.rearrange("(h p) f -> p h f", p=P)).then_inc(s_const, 16)
                    load_x(1, 1)
                    for k, v in enumerate((tok_b, bq, bk)):
                        sp.dma_start(colb[:, k, :], v.rearrange("(h p) -> p h", p=P)).then_inc(s_wts, 16)
                    for k, v in enumerate((bv, bo, gamma, beta)):
                        sp.dma_start(rowb[:, k, :], v.partition_broadcast(TT)).then_inc(s_wts, 16)
                    for dst, v in ((wq_s, wq), (wk_s, wk), (wv_s, wv), (wo_s, wo), (gate_s, gate_w)):
                        sp.dma_start(dst[:], v.rearrange("(k p) n -> p k n", p=P)).then_inc(s_wts, 16)

                    def store(j):
                        sp.wait_ge(s_vc, j + 1)
                        sp.wait_ge(s_qkc, j * 4 + 4)
                        part_waits(sp)
                        sp.dma_start(v_d[bass.ds(j * UT, UT), :].rearrange("(u t) e -> t u e", u=2), vs[:]).then_inc(s_vst, 16)
                        sp.dma_start(qT_d.rearrange("(h p) t -> p h t", p=P)[:, :, bass.ds(j * UT, UT)], qs[:]).then_inc(s_qkst, 16)
                        sp.dma_start(kT_d.rearrange("(h p) t -> p h t", p=P)[:, :, bass.ds(j * UT, UT)], ks[:]).then_inc(s_qkst, 16)

                    def body(i, par, uses):
                        sp.wait_ge(s_xr, (i + 1) * C)
                        if not (isinstance(i, int) and i >= NU - 2):
                            load_x(i + 2, par)
                        if not (isinstance(i, int) and i == 0):
                            store(i - 1)

                    over_units(sp, body)
                    store(NU - 1)
                    sp.wait_ge(s_qkst, 32 * NU)
                    sp.wait_ge(s_vst, 16 * NU)

                @block.gpsimd
                def _(pool):
                    nc.gpsimd.memset(nh[:], -0.5).then_inc(s_nh, 1)
                    pool.wait_ge(s_nh, 1)
                    pool.wait_ge(s_wts, 12 * 16)

                    def body(i, par, uses):
                        pool.wait_ge(s_hve, i + 1)
                        nc.gpsimd.tensor_tensor(rs[:], ve[:], nh[:], ALU.pow).then_inc(s_hrs, 1)
                        pool.wait_ge(s_x1, i + 1)
                        nc.gpsimd.tensor_tensor(x1b[:, bass.ds(i * 2, 2), :], x1s[:], two(bo_bc), ALU.add).then_inc(s_x1b, 1)
                    over_units(pool, body)

                @block.tensor
                def _(pe):
                    pe.wait_ge(s_const, 32)
                    for k in range(KF):
                        for h in range(KD):
                            last = nc.tensor.transpose(bank[k // 2][:, (k % 2) * D + h * P:(k % 2) * D + (h + 1) * P],
                                                       wnat[:, h, k * P:(k + 1) * P], ident)
                    last.then_inc(s_wTt, 1)
                    pe.wait_ge(s_wTc, 3)

                    def patches(i, par, uses):
                        pe.wait_ge(s_xr, (i + 1) * C)
                        pe.wait_ge(s_pTc, i * 3)
                        part_waits(pe)
                        for k in range(KF):
                            for g in range(G):
                                o = (k % 2) * UT + g * UB * G
                                last = nc.tensor.transpose(bank[k // 2][:, o:o + UB * G],
                                                           xr[:, k // 2, g, (k % 2) * P:(k % 2 + 1) * P],
                                                           ident[0:UB * G, 0:UB * G])
                            last.then_inc(s_pT, 1)

                    def turn_normed(j):
                        pe.wait_ge(s_x1, j + 1)
                        pe.wait_ge(s_vc, j)
                        for h in range(KD):
                            for u in range(2):
                                last = nc.tensor.transpose(x1T_ps[:, h * UT + u * TT:h * UT + (u + 1) * TT],
                                                           x1s[:, u, h * P:(h + 1) * P], ident[0:TT, 0:TT])
                        last.then_inc(s_x1T, 1)

                    def project(j):
                        pe.wait_ge(s_x1Tc, j + 1)
                        for u in range(2):
                            for k in range(KD):
                                last = nc.tensor.matmul(v_ps[0:TT, u * D:(u + 1) * D], x1Ts[:, k, u * TT:(u + 1) * TT],
                                                        wv_s[:, k, :], start=(k == 0), stop=(k == KD - 1))
                        last.then_inc(s_v, 1)
                        pe.wait_ge(s_qkc, j * 4)
                        for w, ps in ((wq_s, q_ps), (wk_s, k_ps)):
                            for h in range(KD):
                                for k in range(KD):
                                    last = nc.tensor.matmul(ps[:, h * UT:(h + 1) * UT], w[:, k, h * P:(h + 1) * P],
                                                            x1Ts[:, k, :], start=(k == 0), stop=(k == KD - 1))
                            last.then_inc(s_qk, 1)

                    def body(i, par, uses):
                        lag = not (isinstance(i, int) and i == 0)
                        pe.wait_ge(s_pTc, (i + 1) * 3)
                        for h in range(KD):
                            for k in range(KF):
                                last = nc.tensor.matmul(hT_ps[:, h * UT:(h + 1) * UT], wT[:, k, h * P:(h + 1) * P],
                                                        pT[:, k, :], start=(k == 0), stop=(k == KF - 1))
                        last.then_inc(s_hT, 1)
                        if lag:
                            turn_normed(i - 1)
                        if not last_unit(i):
                            patches(i + 1, 1 - par, uses + par)
                        pe.wait_ge(s_hTc, (i + 1) * 2)
                        pe.wait_ge(s_hb, i)
                        pe.wait_ge(s_x1, i)
                        for u in range(2):
                            for h in range(KD):
                                last = nc.tensor.transpose(h_ps[0:TT, u * D + h * P:u * D + (h + 1) * P],
                                                           hTs[:, h, u * TT:(u + 1) * TT], ident)
                        last.then_inc(s_h, 1)
                        if lag:
                            project(i - 1)

                    patches(0, 0, 1)
                    pe.wait_ge(s_wts, 12 * 16)
                    over_units(pe, body)
                    turn_normed(NU - 1)
                    project(NU - 1)

                @block.scalar
                def _(act):
                    act.wait_ge(s_wTt, 1)
                    for k in range(3):
                        nc.scalar.activation(wT[:, 2 * k:2 * k + 2, :], bank[k][:].rearrange("p (k n) -> p k n", k=2),
                                             ACT.Copy).then_inc(s_wTc, 1)

                    def patches(i):
                        for k in range(3):
                            act.wait_ge(s_pT, i * KF + 2 * k + 2)
                            src = bank[k][:, 0:2 * UT].rearrange("p (k g r) -> p k g r", k=2, g=G)
                            dst = pT[:, 2 * k:2 * k + 2, :].rearrange("p k (r g) -> p k g r", g=G)
                            for h in range(2):
                                last = nc.scalar.activation(dst[:, h], src[:, h], ACT.Copy)
                            last.then_inc(s_pTc, 1)

                    def copy_normed(j):
                        act.wait_ge(s_x1T, j + 1)
                        nc.scalar.activation(x1Ts[:], x1T_ps[:, 0:2 * UT].rearrange("p (k t) -> p k t", k=2),
                                             ACT.Copy).then_inc(s_x1Tc, 1)

                    def queries_keys(j):
                        act.wait_ge(s_qkst, j * 32)
                        for n, (dst, ps, scale) in enumerate(((qs, q_ps, HD ** -0.5), (ks, k_ps, 1.0))):
                            act.wait_ge(s_qk, j * 2 + n + 1)
                            for h in range(KD):
                                nc.scalar.activation(dst[:, h, :], ps[:, h * UT:(h + 1) * UT], ACT.Identity,
                                                     bias=colb[:, n + 1, h:h + 1], scale=scale).then_inc(s_qkc, 1)

                    def body(i, par, uses):
                        lag = not (isinstance(i, int) and i == 0)
                        act.wait_ge(s_hT, i + 1)
                        for h in range(KD):
                            nc.scalar.activation(hTs[:, h, :], hT_ps[:, h * UT:(h + 1) * UT], ACT.Identity,
                                                 bias=colb[:, 0, h:h + 1]).then_inc(s_hTc, 1)
                        if lag:
                            copy_normed(i - 1)
                        if not last_unit(i):
                            patches(i + 1)
                        if lag:
                            queries_keys(i - 1)

                    patches(0)
                    act.wait_ge(s_wts, 12 * 16)
                    act.wait_ge(s_bq4, 1)
                    over_units(act, body)
                    copy_normed(NU - 1)
                    queries_keys(NU - 1)

                @block.vector
                def _(dve):
                    def regroup(i, par, uses):
                        dve.wait_ge(s_x[par], uses * 16 * C)
                        dve.wait_ge(s_pT, i * KF)
                        for c in range(C):
                            nc.vector.tensor_copy(xr[:, c].rearrange("p g (r w) -> p g r w", w=PATCH),
                                                  xraw[par][:, c].rearrange("p (r g w) -> p g r w", g=G, w=PATCH)).then_inc(s_xr, 1)

                    regroup(0, 0, 1)
                    dve.wait_ge(s_wts, 12 * 16)
                    nc.vector.tensor_scalar(colb[:, 1, :], colb[:, 1, :], HD ** -0.5, None, ALU.mult).then_inc(s_bq4, 1)

                    def copy_values(j):
                        dve.wait_ge(s_v, j + 1)
                        dve.wait_ge(s_vst, j * 16)
                        nc.vector.tensor_tensor(vs[:], v_ps[0:TT, :].rearrange("p (u e) -> p u e", u=2), two(bv_bc),
                                                ALU.add).then_inc(s_vc, 1)

                    def body(i, par, uses):
                        if not last_unit(i):
                            regroup(i + 1, 1 - par, uses + par)
                        dve.wait_ge(s_h, i + 1)
                        for u in range(2):
                            nc.vector.bn_stats(st[:, u, :], h_ps[0:TT, u * D:(u + 1) * D]).then_inc(s_hbn, 1)
                        nc.vector.tensor_tensor(hb[:, bass.ds(i * 2, 2), :], h_ps[0:TT, :].rearrange("p (u e) -> p u e", u=2),
                                                two(be_bc), ALU.add).then_inc(s_hb, 1)
                        dve.wait_ge(s_hbn, (i + 1) * 2)
                        part_waits(dve)
                        for u in range(2):
                            nc.vector.bn_aggr(mv[:, u, :], st[:, u, :]).then_inc(s_hag, 1)
                        dve.wait_ge(s_hag, (i + 1) * 2)
                        nc.vector.tensor_scalar(ve[:], mv[:, :, 1], LN_EPS, None, ALU.add).then_inc(s_hve, 1)
                        if not (isinstance(i, int) and i == 0):
                            copy_values(i - 1)
                        dve.wait_ge(s_hrs, i + 1)
                        dve.wait_ge(s_x1b, i)
                        for u in range(2):
                            last = nc.vector.tensor_scalar(x1s[:, u, :], h_ps[0:TT, u * D:(u + 1) * D], mv[:, u, 0:1],
                                                           rs[:, u:u + 1], ALU.subtract, ALU.mult)
                        last.then_inc(s_x1, 1)
                    over_units(dve, body)
                    copy_values(NU - 1)

        s_q_in = [sem("qk_in0"), sem("qk_in1")]
        s_v_in = [sem("v_in0"), sem("v_in1")]
        s_z, s_one, s_zb, s_pad = sem("values_zeroed"), sem("value_ones"), sem("banks_zeroed"), sem("padding_zeroed")
        s_Qc, s_Kc, s_Kbd = sem("Q_ordered"), sem("K_ordered"), sem("K_blocked")
        s_S, s_red, s_sub, s_exp = sem("scores_done"), sem("max_done"), sem("max_subtracted"), sem("exp_done")
        s_T, s_Tc, s_PV, s_rc, s_ctx = sem("probs_turned"), sem("probsT_copied"), sem("PV_done"), sem("rec_done"), sem("ctx_done")
        s_cst = [sem("ctx_stored0"), sem("ctx_stored1")]

        with ExitStack() as ctx:
            qst = [sb(ctx, f"qst{k}", [P, HEADS, N]) for k in range(2)]
            kst = [sb(ctx, f"kst{k}", [P, HEADS, N]) for k in range(2)]
            vb = [sb(ctx, f"vb{k}", [TT, 3, HEADS, 3, HD + 1]) for k in range(2)]
            Qc = [sb(ctx, f"Qc{k}", [P, HEADS * N]) for k in range(2)]
            Kc = sb(ctx, "Kc", [P, HEADS * N])
            Kbd = [sb(ctx, f"Kbd{k}", [P, HEADS, AB, N]) for k in range(2)]
            mx = [sb(ctx, f"mx{k}", [P, AB]) for k in range(2)]
            pr = [sb(ctx, f"probs{k}", [P, AB * N]) for k in range(2)]
            pT = [sb(ctx, f"probsT{k}", [TT, 3 * P]) for k in range(2)]
            rc = [sb(ctx, f"rc{k}", [P, AB]) for k in range(2)]
            cs = [sb(ctx, f"cs{k}", [P, AI, AB, HD]) for k in range(2)]
            pad = sb(ctx, "pad", [T - B * N, D])
            SC, PT, PV = bank[0:2], bank[2:4], bank[4:6]
            width = [TT, TT, (AB - 6) * N]

            def item(i, par, m):
                if m < AI:
                    return i, par, m
                return None if isinstance(i, int) and i == AU - 1 else (i + 1, 1 - par, m - AI)

            with nc.Block() as block:
                @block.sync
                def _(sp):
                    def load(i, par):
                        for s in range(AB):
                            t0 = (i * AB + s) * N
                            sp.dma_start(qst[par][HD * s:HD * s + HD], q_view[:, :, bass.ds(t0, N)]).then_inc(s_q_in[par], 16)
                            sp.dma_start(kst[par][HD * s:HD * s + HD], k_view[:, :, bass.ds(t0, N)]).then_inc(s_q_in[par], 16)
                    load(0, 0)
                    load(1, 1)
                    sp.wait_ge(s_pad, 1)
                    sp.dma_start(c_d[B * N:T, :], pad[:]).then_inc(s_cst[0], 16)

                    def body(i, par, uses):
                        if not (isinstance(i, int) and i >= AU - 2):
                            sp.wait_ge(s_Kc, i + 1)
                            sp.wait_ge(s_Qc, i + 1)
                            load(i + 2, par)
                        sp.wait_ge(s_ctx, (i + 1) * AI)
                        for s in range(AB):
                            for h in range(2):
                                dst = c_view[bass.ds(i * AB + s, 1), :, h].rearrange("o m q d -> q (o m) d")
                                sp.dma_start(dst, cs[par][64 * h:64 * h + N, :, s, :]).then_inc(s_cst[par], 16)
                    over_units(sp, body, AU)
                    sp.wait_ge(s_cst[0], AU // 2 * CST + 16)
                    sp.wait_ge(s_cst[1], AU // 2 * CST)

                @block.gpsimd
                def _(pool):
                    def load(i, par):
                        for s in range(AB):
                            t0 = (i * AB + s) * N
                            src = v_flat[bass.ds(t0 * D, N * D)].rearrange("(g k d) -> k g d", k=N, d=HD)
                            r0 = s % 3 * N
                            pool.dma_start(vb[par][r0:r0 + N, s // 3, :, s % 3, 0:HD], src).then_inc(s_v_in[par], 16)

                    def block_keys(i, par):
                        mask = mk[:, M_M8:M_M8 + AB].unsqueeze(1).unsqueeze(3).to_broadcast([P, 4, AB, N])
                        kg = Kc[:].rearrange("p (g k) -> p g k", k=N)
                        for q in range(4):
                            nc.gpsimd.tensor_tensor(Kbd[par][:, 4 * q:4 * q + 4], mask,
                                                    kg[:, 4 * q:4 * q + 4, :].unsqueeze(2).to_broadcast([P, 4, AB, N]),
                                                    ALU.mult).then_inc(s_Kbd, 1)
                    nc.gpsimd.memset(pad[:], 0.0).then_inc(s_pad, 1)
                    for k in range(2):
                        nc.gpsimd.memset(vb[k][:], 0.0).then_inc(s_z, 1)
                    pool.wait_ge(s_one, 2)
                    load(0, 0)
                    load(1, 1)
                    pool.wait_ge(s_Kc, 1)
                    block_keys(0, 0)

                    def body(i, par, uses):
                        if not (isinstance(i, int) and i == AU - 1):
                            pool.wait_ge(s_Kc, i + 2)
                            pool.wait_ge(s_S, i * AI)
                            block_keys(i + 1, 1 - par)
                        if not (isinstance(i, int) and i >= AU - 2):
                            pool.wait_ge(s_PV, (i + 1) * AI)
                            part_waits(pool)
                            load(i + 2, par)
                    over_units(pool, body, AU)

                @block.vector
                def _(dve):
                    def order(i, par, uses):
                        dve.wait_ge(s_q_in[par], uses * 2 * AB * 16)
                        dve.wait_ge(s_Kbd, i * 4)
                        nc.vector.tensor_copy(Kc[:].rearrange("p (t j) -> p t j", j=HEADS),
                                              kst[par][:].rearrange("p j t -> p t j")).then_inc(s_Kc, 1)
                        if not (isinstance(i, int) and i < 2):
                            dve.wait_ge(s_S, (i - 1) * AI)
                        nc.vector.tensor_copy(Qc[par][:].rearrange("p (t j) -> p t j", j=HEADS),
                                              qst[par][:].rearrange("p j t -> p t j")).then_inc(s_Qc, 1)

                    def subtract_max(i, par, m):
                        n, b = i * AI + m, m % 2
                        sc = SC[b][:, 0:AB * N].rearrange("p (s k) -> p s k", k=N)
                        dve.wait_ge(s_S, n + 1)
                        nc.vector.tensor_reduce(mx[b][:], sc, AX, ALU.max).then_inc(s_red, 1)
                        dve.wait_ge(s_red, n + 1)
                        if not (isinstance(n, int) and n < 2):
                            dve.wait_ge(s_T, n - 1)
                        nc.vector.tensor_tensor(pr[b][:].rearrange("p (s k) -> p s k", k=N), sc,
                                                mx[b][:].unsqueeze(2).to_broadcast([P, AB, N]), ALU.subtract).then_inc(s_sub, 1)

                    def context(i, par, m, uses):
                        n, b = i * AI + m, m % 2
                        pv = PV[b][:, 0:AB * (HD + 1)].rearrange("p (s d) -> p s d", d=HD + 1)
                        dve.wait_ge(s_PV, n + 1)
                        nc.vector.reciprocal(rc[b][:], pv[:, :, HD]).then_inc(s_rc, 1)
                        dve.wait_ge(s_rc, n + 1)
                        if m == 0:
                            dve.wait_ge(s_cst[par], (uses - 1) * CST + 16 * (1 - par))
                        nc.vector.tensor_tensor(cs[par][:, m], pv[:, :, 0:HD], rc[b][:].unsqueeze(2).to_broadcast([P, AB, HD]),
                                                ALU.mult).then_inc(s_ctx, 1)

                    def body(i, par, uses):
                        for m in range(AI):
                            nxt2 = item(i, par, m + 2)
                            if nxt2:
                                subtract_max(*nxt2)
                            context(i, par, m, uses)
                            if m == 0 and not (isinstance(i, int) and i == AU - 1):
                                order(i + 1, 1 - par, uses + par)
                    for k in range(6):
                        fill = 1.0 if k in (4, 5) else 0.0
                        nc.vector.memset(bank[k][:], fill).then_inc(s_zb, 1)
                    dve.wait_ge(s_z, 2)
                    for k in range(2):
                        ones = mk[0:TT, M_A3:M_A3 + 3].unsqueeze(1).to_broadcast([TT, 3 * HEADS, 3])
                        nc.vector.tensor_copy(vb[k][:, :, :, :, HD].rearrange("p c g s -> p (c g) s"), ones).then_inc(s_one, 1)
                    dve.wait_ge(s_zb, 6)
                    order(0, 0, 1)
                    subtract_max(0, 0, 0)
                    subtract_max(0, 0, 1)
                    over_units(dve, body, AU)

                @block.scalar
                def _(act):
                    def exponent(i, par, m):
                        act.wait_ge(s_sub, i * AI + m + 1)
                        nc.scalar.activation(pr[m % 2][:], pr[m % 2][:], ACT.Exp).then_inc(s_exp, 1)

                    def copy_turned(i, par, m):
                        n = i * AI + m
                        act.wait_ge(s_T, n + 1)
                        if not (isinstance(n, int) and n < 2):
                            act.wait_ge(s_PV, n - 1)
                        nc.scalar.activation(pT[m % 2][:], PT[m % 2][0:TT, 0:3 * P], ACT.Copy).then_inc(s_Tc, 1)

                    def body(i, par, uses):
                        for m in range(AI):
                            nxt, nxt2 = item(i, par, m + 1), item(i, par, m + 2)
                            if nxt:
                                copy_turned(*nxt)
                            if nxt2:
                                exponent(*nxt2)
                    exponent(0, 0, 0)
                    exponent(0, 0, 1)
                    copy_turned(0, 0, 0)
                    over_units(act, body, AU)

                @block.tensor
                def _(pe):
                    def scores(i, par, m):
                        n, b = i * AI + m, m % 2
                        if m == 0:
                            pe.wait_ge(s_Qc, i + 1)
                        if m % 2 == 0:
                            pe.wait_ge(s_Kbd, i * 4 + m // 2 + 1)
                        if not (isinstance(n, int) and n < 2):
                            pe.wait_ge(s_sub, n - 1)
                        for h in range(2):
                            g = 2 * m + h
                            last = nc.tensor.matmul(SC[b][64 * h:64 * h + N, 0:AB * N], Qc[par][:, g * N:(g + 1) * N],
                                                    Kbd[par][:, g].rearrange("p s k -> p (s k)"), start=True, stop=True)
                        last.then_inc(s_S, 1)

                    def turn(i, par, m):
                        n, b = i * AI + m, m % 2
                        pe.wait_ge(s_exp, n + 1)
                        if not (isinstance(n, int) and n < 2):
                            pe.wait_ge(s_Tc, n - 1)
                        for c in range(3):
                            last = nc.tensor.transpose(PT[b][0:width[c], c * P:(c + 1) * P],
                                                       pr[b][:, c * TT:c * TT + width[c]], ident)
                        last.then_inc(s_T, 1)

                    def values(i, par, m):
                        n, b = i * AI + m, m % 2
                        pe.wait_ge(s_Tc, n + 1)
                        if not (isinstance(n, int) and n < 2):
                            pe.wait_ge(s_ctx, n - 1)
                        for h in range(2):
                            for c in range(3):
                                w, k = width[c], width[c] // N * (HD + 1)
                                last = nc.tensor.matmul(PV[b][64 * h:64 * h + N, 51 * c:51 * c + k],
                                                        pT[b][0:w, c * P + 64 * h:c * P + 64 * h + N],
                                                        vb[par][0:w, c, 2 * m + h].rearrange("p s d -> p (s d)")[:, 0:k],
                                                        start=True, stop=True)
                        last.then_inc(s_PV, 1)

                    def body(i, par, uses):
                        for m in range(AI):
                            nxt, nxt2 = item(i, par, m + 1), item(i, par, m + 2)
                            if nxt2:
                                scores(*nxt2)
                            if nxt:
                                turn(*nxt)
                            if m == 0:
                                pe.wait_ge(s_v_in[par], uses * AB * 16)
                            values(i, par, m)
                    pe.wait_ge(s_zb, 6)
                    scores(0, 0, 0)
                    scores(0, 0, 1)
                    turn(0, 0, 0)
                    over_units(pe, body, AU)

        s_c_in = [sem("ctx_in0"), sem("ctx_in1")]
        names = ("c_turned c_copied o_done r_done r_bn r_ag r_ve r_rs n1_done h2_done h2_bn h2_ag h2_ve h2_rs h2_nm x2_done "
                 "x2T_done x2T_copied g_done g_max g_sub g_exp g_sum g_rec p_done X_done Bp_done gt_done eq_done "
                 "eqL_done cnt_done rank_done S_done SP_done xin_done xin_copied SPT_done SPT_copied SPT_stored").split()
        S = {n: sem(n) for n in names}
        s_w1, s_w2 = sem("w1_in"), sem("w2_in")
        s_zy, s_low = sem("xin_zeroed"), sem("low_bf16")
        BF16 = mybir.dt.bfloat16
        xinT = sb(top, "xinT", [P, KD, E, PSLOTS])
        w1s = sb(top, "w1s", [P, KD, HID])
        w2s = sb(top, "w2s", [P, KH, D])

        with ExitStack() as ctx:
            cN = [sb(ctx, f"cN{k}", [TT, 2, D]) for k in range(2)]
            cT = [sb(ctx, f"cT{k}", [P, KD, UT]) for k in range(2)]
            r = sb(ctx, "r", [TT, 2, D])
            n1 = sb(ctx, "n1", [TT, 2, D])
            x2 = [sb(ctx, f"x2_{k}", [TT, 2, D]) for k in range(2)]
            x2T = sb(ctx, "x2T", [P, KD, UT])
            stA, stB = sb(ctx, "stA", [TT, 2, 6]), sb(ctx, "stB", [TT, 2, 6])
            mvA, mvB = sb(ctx, "mvA", [TT, 2, 2]), sb(ctx, "mvB", [TT, 2, 2])
            rsA, rsB = sb(ctx, "rsA", [TT, 2]), sb(ctx, "rsB", [TT, 2])
            veA, veB = sb(ctx, "veA", [TT, 2]), sb(ctx, "veB", [TT, 2])
            nm = sb(ctx, "nm", [TT, 2])
            gm = sb(ctx, "gm", [TT, 2])
            gs = sb(ctx, "gs", [TT, 2])
            gr = sb(ctx, "gr", [TT, 2])
            ge = sb(ctx, "ge", [TT, 2, E])
            pr = [sb(ctx, f"pr{k}", [TT, 2, E]) for k in range(2)]
            X = sb(ctx, "X", [TT, 2, E, N])
            gt, eq = (ctx.enter_context(nc.sbuf_tensor(n, [TT, 2, E, N], BF16)) for n in ("gt", "eq"))
            lowb = ctx.enter_context(nc.sbuf_tensor("lowb", [TT, E, N], BF16))
            rank = sb(ctx, "rank", [TT, 2, E])
            Sm = sb(ctx, "Sm", [TT, 2, E, TS])
            SP = sb(ctx, "SP", [TT, 2, E, TS])
            SPTs = sb(ctx, "SPTs", [TT, 2, 2 * TT])
            o_ps, x2T_ps, cT_ps, B_ps, xin_ps, spt_ps = bank[0], bank[1], bank[2], bank[3:5], bank[5:7], bank[7]
            g_ps = cT_ps[0:TT, 2 * UT:2 * UT + 2 * E]

            def stages(i):
                return [not isinstance(i, int) or 0 <= i - k < NU for k in range(3)]

            def over_stages(eng, body):
                over_units(eng, body)
                body(NU, NU % 2, NU // 2 + 1)
                body(NU + 1, (NU + 1) % 2, (NU + 1) // 2 + 1)

            with nc.Block() as block:
                def halves(ap):
                    return ap.rearrange("p (u e) -> p u e", u=2)


                @block.sync
                def _(sp):
                    def load(i, par):
                        src = c_d[bass.ds(i * UT, UT), :].rearrange("(u t) e -> t u e", u=2)
                        sp.dma_start(cN[par][:], src).then_inc(s_c_in[par], 16)
                    load(0, 0)
                    load(1, 1)
                    sp.dma_start(w1s[:], w1[0].rearrange("(k p) n -> p k n", p=P)).then_inc(s_w1, 16)
                    sp.dma_start(w2s[:], w2[0].rearrange("(k p) n -> p k n", p=P)).then_inc(s_w2, 16)

                    def body(i, par, uses):
                        if not (isinstance(i, int) and i >= NU - 2):
                            sp.wait_ge(S["c_turned"], i + 1)
                            load(i + 2, par)
                    over_units(sp, body)
                    sp.wait_ge(S["SPT_stored"], NU * 16)

                @block.gpsimd
                def _(pool):
                    i36 = mk[0:TT, M_I36:M_I36 + N].unsqueeze(1).to_broadcast([TT, E, N])

                    def norms(i):
                        pool.wait_ge(S["r_ve"], i + 1)
                        nc.gpsimd.tensor_tensor(rsA[:], veA[:], nh[:], ALU.pow).then_inc(S["r_rs"], 1)
                        pool.wait_ge(S["h2_ve"], i + 1)
                        pool.wait_ge(S["x2_done"], i)
                        nc.gpsimd.tensor_tensor(rsB[:], veB[:], nh[:], ALU.pow).then_inc(S["h2_rs"], 1)

                    def spreadable(j, par):
                        pool.wait_ge(S["p_done"], j + 1)
                        pool.wait_ge(S["Bp_done"], j * 2)
                        for u in range(2):
                            nc.gpsimd.tensor_tensor(X[:, u], pr[par][:, u, :].unsqueeze(2).to_broadcast([TT, E, N]), i36,
                                                    ALU.mult).then_inc(S["X_done"], 1)

                    def weighted_slots(j, par):
                        pool.wait_ge(S["SPT_done"], j)
                        for u in range(2):
                            pool.wait_ge(S["S_done"], j * 2 + u + 1)
                            nc.gpsimd.tensor_tensor(SP[:, u], Sm[:, u], pr[par][:, u, :].unsqueeze(2).to_broadcast([TT, E, TS]),
                                                    ALU.mult).then_inc(S["SP_done"], 1)

                    def body(i, par, uses):
                        here, one, two = stages(i)
                        if here:
                            norms(i)
                        if two:
                            weighted_slots(i - 2, par)
                        if one:
                            spreadable(i - 1, 1 - par)
                    over_stages(pool, body)

                @block.vector
                def _(dve):
                    def stats(i, src, st, mv, ve, name):
                        for u in range(2):
                            nc.vector.bn_stats(st[:, u, :], src[:, u, :]).then_inc(S[name + "_bn"], 1)
                        dve.wait_ge(S[name + "_bn"], (i + 1) * 2)
                        part_waits(dve)
                        for u in range(2):
                            nc.vector.bn_aggr(mv[:, u, :], st[:, u, :]).then_inc(S[name + "_ag"], 1)
                        dve.wait_ge(S[name + "_ag"], (i + 1) * 2)
                        nc.vector.tensor_scalar(ve[:], mv[:, :, 1], LN_EPS, None, ALU.add).then_inc(S[name + "_ve"], 1)

                    def residual(i):
                        dve.wait_ge(S["o_done"], i + 1)
                        nc.vector.tensor_tensor(r[:], halves(o_ps[0:TT, :]), x1b[:, bass.ds(i * 2, 2), :], ALU.add).then_inc(S["r_done"], 1)
                        dve.wait_ge(S["r_done"], i + 1)
                        stats(i, r, stA, mvA, veA, "r")
                        for u in range(2):
                            nc.vector.scalar_tensor_tensor(out=n1[:, u, :], in0=r[:, u, :], scalar=mvA[:, u, 0:1], in1=ga_bc,
                                                           op0=ALU.subtract, op1=ALU.mult).then_inc(S["n1_done"], 1)

                    def stream(i):
                        dve.wait_ge(S["r_rs"], i + 1)
                        dve.wait_ge(S["n1_done"], (i + 1) * 2)
                        for u in range(2):
                            hu = hb[:, bass.ds(i * 2 + u, 1), :].squeeze(1)
                            nc.vector.scalar_tensor_tensor(out=hu, in0=n1[:, u, :], scalar=rsA[:, u:u + 1], in1=hu,
                                                           op0=ALU.mult, op1=ALU.add).then_inc(S["h2_done"], 1)
                        dve.wait_ge(S["h2_done"], (i + 1) * 2)
                        part_waits(dve)
                        stats(i, hb[:, bass.ds(i * 2, 2), :], stB, mvB, veB, "h2")

                    def shift(i):
                        dve.wait_ge(S["h2_rs"], i + 1)
                        dve.wait_ge(S["x2_done"], i)
                        nc.vector.scalar_tensor_tensor(out=nm[:], in0=mvB[:, :, 0], scalar=-1.0, in1=rsB[:],
                                                       op0=ALU.mult, op1=ALU.mult).then_inc(S["h2_nm"], 1)

                    gps = g_ps.rearrange("p (u e) -> p u e", u=2)

                    def gate_max(j):
                        dve.wait_ge(S["g_done"], j + 1)
                        nc.vector.tensor_reduce(gm[:], gps, AX, ALU.max).then_inc(S["g_max"], 1)
                        dve.wait_ge(S["g_max"], j + 1)
                        nc.vector.tensor_tensor(ge[:], gps, gm[:].unsqueeze(2).to_broadcast([TT, 2, E]),
                                                ALU.subtract).then_inc(S["g_sub"], 1)

                    def gate_probs(j, par):
                        dve.wait_ge(S["g_exp"], j + 1)
                        nc.vector.tensor_reduce(gs[:], ge[:], AX, ALU.add).then_inc(S["g_sum"], 1)
                        dve.wait_ge(S["g_sum"], j + 1)
                        nc.vector.reciprocal(gr[:], gs[:]).then_inc(S["g_rec"], 1)
                        dve.wait_ge(S["g_rec"], j + 1)
                        if not (isinstance(j, int) and j < 2):
                            dve.wait_ge(S["SP_done"], (j - 1) * 2)
                        nc.vector.tensor_tensor(pr[par][:], ge[:], gr[:].unsqueeze(2).to_broadcast([TT, 2, E]),
                                                ALU.mult).then_inc(S["p_done"], 1)

                    def compare(j, par):
                        for u in range(2):
                            dve.wait_ge(S["Bp_done"], j * 2 + u + 1)
                            bp = B_ps[u][0:TT, 0:E * N].rearrange("p (e t) -> p e t", e=E)
                            own = pr[par][:, u, :].unsqueeze(2).to_broadcast([TT, E, N])
                            nc.vector.tensor_tensor(eq[:, u], bp, own, ALU.is_equal).then_inc(S["eq_done"], 1)
                            nc.vector.tensor_tensor(gt[:, u], bp, own, ALU.is_gt).then_inc(S["gt_done"], 1)

                    def count(j):
                        for u in range(2):
                            dve.wait_ge(S["eq_done"], j * 2 + u + 1)
                            nc.vector.tensor_tensor(eq[:, u], eq[:, u], lowb[:], ALU.mult).then_inc(S["eqL_done"], 1)
                        for u in range(2):
                            dve.wait_ge(S["gt_done"], j * 2 + u + 1)
                            dve.wait_ge(S["eqL_done"], j * 2 + u + 1)
                            nc.vector.tensor_tensor(gt[:, u], gt[:, u], eq[:, u], ALU.add).then_inc(S["cnt_done"], 1)

                    def slots(j):
                        for u in range(2):
                            dve.wait_ge(S["cnt_done"], j * 2 + u + 1)
                            nc.vector.tensor_reduce(rank[:, u, :], gt[:, u], AX, ALU.add).then_inc(S["rank_done"], 1)
                        iota = mk[0:TT, M_IOTA:M_IOTA + TS].unsqueeze(1).to_broadcast([TT, E, TS])
                        dve.wait_ge(S["xin_done"], j * 2)
                        dve.wait_ge(S["SP_done"], j * 2)
                        for u in range(2):
                            dve.wait_ge(S["rank_done"], j * 2 + u + 1)
                            nc.vector.tensor_tensor(Sm[:, u], rank[:, u, :].unsqueeze(2).to_broadcast([TT, E, TS]), iota,
                                                    ALU.is_equal).then_inc(S["S_done"], 1)

                    def body(i, par, uses):
                        here, one, two = stages(i)
                        if here:
                            residual(i)
                            stream(i)
                        if two:
                            compare(i - 2, par)
                        if here:
                            shift(i)
                        if two:
                            count(i - 2)
                        if one:
                            gate_max(i - 1)
                        if two:
                            slots(i - 2)
                        if one:
                            gate_probs(i - 1, 1 - par)

                    nc.vector.memset(xinT[:, :, :, SLOTS:PSLOTS], 0.0).then_inc(s_zy, 1)
                    nc.vector.tensor_copy(lowb[:], mk[0:TT, M_LOW:M_LOW + N].unsqueeze(1).to_broadcast([TT, E, N])).then_inc(s_low, 1)
                    dve.wait_ge(s_low, 1)
                    over_stages(dve, body)

                @block.scalar
                def _(act):
                    def gate_exp(j):
                        act.wait_ge(S["g_sub"], j + 1)
                        nc.scalar.activation(ge[:], ge[:], ACT.Exp).then_inc(S["g_exp"], 1)

                    def norm(i, par):
                        act.wait_ge(S["h2_nm"], i + 1)
                        if not (isinstance(i, int) and i < 2):
                            act.wait_ge(S["xin_done"], (i - 1) * 2)
                        for u in range(2):
                            last = nc.scalar.activation(x2[par][:, u, :], hb[:, bass.ds(i * 2 + u, 1), :].squeeze(1), ACT.Identity,
                                                        bias=nm[:, u:u + 1], scale=rsB[:, u:u + 1])
                        last.then_inc(S["x2_done"], 1)

                    def gathered(j):
                        for u in range(2):
                            act.wait_ge(S["xin_done"], j * 2 + u + 1)
                            for h in range(KD):
                                last = nc.scalar.activation(xinT[:, h, :, bass.ds((j * 2 + u) * TS, TS)],
                                                            xin_ps[u][:, h * E * TS:(h + 1) * E * TS].rearrange("p (e s) -> p e s", e=E),
                                                            ACT.Copy)
                            last.then_inc(S["xin_copied"], 1)
                        act.wait_ge(S["SPT_done"], j + 1)
                        act.wait_ge(S["SPT_stored"], j * 16)
                        nc.scalar.activation(SPTs[:], spt_ps[0:TT, 0:4 * TT].rearrange("p (u n) -> p u n", u=2),
                                             ACT.Copy).then_inc(S["SPT_copied"], 1)
                        act.wait_ge(S["SPT_copied"], j + 1)
                        part_waits(act)
                        act.dma_start(spt_d[bass.ds(j * 2, 2)].rearrange("u p n -> p u n"), SPTs[:]).then_inc(S["SPT_stored"], 16)

                    def copy_context(i, par):
                        act.wait_ge(S["c_turned"], i + 1)
                        if not (isinstance(i, int) and i < 2):
                            act.wait_ge(S["o_done"], i - 1)
                        nc.scalar.activation(cT[par][:], cT_ps[:, 0:2 * UT].rearrange("p (k t) -> p k t", k=2),
                                             ACT.Copy).then_inc(S["c_copied"], 1)

                    def body(i, par, uses):
                        here, one, two = stages(i)
                        if not (isinstance(i, int) and i >= NU - 2):
                            copy_context(i + 2, par)
                        if one:
                            gate_exp(i - 1)
                        if here:
                            norm(i, par)
                        if two:
                            gathered(i - 2)
                        if here:
                            act.wait_ge(S["x2T_done"], i + 1)
                            nc.scalar.activation(x2T[:], x2T_ps[:, 0:2 * UT].rearrange("p (k t) -> p k t", k=2),
                                                 ACT.Copy).then_inc(S["x2T_copied"], 1)
                    copy_context(0, 0)
                    copy_context(1, 1)
                    act.wait_ge(s_zy, 1)
                    over_stages(act, body)

                @block.tensor
                def _(pe):
                    def turn_context(i, par, uses):
                        pe.wait_ge(s_c_in[par], uses * 16)
                        pe.wait_ge(S["c_copied"], i)
                        if not (isinstance(i, int) and i < 4):
                            pe.wait_ge(S["g_sub"], i - 3)
                        for h in range(KD):
                            for u in range(2):
                                last = nc.tensor.transpose(cT_ps[:, h * UT + u * TT:h * UT + (u + 1) * TT],
                                                           cN[par][:, u, h * P:(h + 1) * P], ident[0:TT, 0:TT])
                        last.then_inc(S["c_turned"], 1)

                    def project(i, par, uses):
                        pe.wait_ge(S["c_copied"], i + 1)
                        pe.wait_ge(S["r_done"], i)
                        for u in range(2):
                            for k in range(KD):
                                last = nc.tensor.matmul(o_ps[0:TT, u * D:(u + 1) * D], cT[par][:, k, u * TT:(u + 1) * TT],
                                                        wo_s[:, k, :], start=(k == 0), stop=(k == KD - 1))
                        last.then_inc(S["o_done"], 1)

                    def gate(j):
                        pe.wait_ge(S["x2T_copied"], j + 1)
                        pe.wait_ge(S["g_sub"], j)
                        pe.wait_ge(S["c_copied"], min(j + 4, NU) if isinstance(j, int) else j + 4)
                        for u in range(2):
                            for k in range(KD):
                                last = nc.tensor.matmul(g_ps[:, u * E:(u + 1) * E], x2T[:, k, u * TT:(u + 1) * TT],
                                                        gate_s[:, k, :], start=(k == 0), stop=(k == KD - 1))
                        last.then_inc(S["g_done"], 1)

                    def spread(j):
                        pe.wait_ge(S["gt_done"], j * 2)
                        for u in range(2):
                            pe.wait_ge(S["X_done"], j * 2 + u + 1)
                            nc.tensor.matmul(B_ps[u][0:TT, 0:E * N], mk[0:TT, M_BLK:M_BLK + TT],
                                             X[:, u].rearrange("p e t -> p (e t)"), start=True, stop=True).then_inc(S["Bp_done"], 1)

                    def gather(j, par):
                        pe.wait_ge(S["xin_copied"], j * 2)
                        for u in range(2):
                            pe.wait_ge(S["S_done"], j * 2 + u + 1)
                            for h in range(KD):
                                last = nc.tensor.matmul(xin_ps[u][:, h * E * TS:(h + 1) * E * TS], x2[par][:, u, h * P:(h + 1) * P],
                                                        Sm[:, u].rearrange("p e s -> p (e s)"), start=True, stop=True)
                            last.then_inc(S["xin_done"], 1)

                    def turn_slots(j):
                        pe.wait_ge(S["SP_done"], j * 2 + 2)
                        pe.wait_ge(S["SPT_copied"], j)
                        for u in range(2):
                            for q in range(2):
                                last = nc.tensor.transpose(spt_ps[0:TT, (2 * u + q) * TT:(2 * u + q + 1) * TT],
                                                           SP[:, u, 4 * q:4 * q + 4, :].rearrange("p e s -> p (e s)"),
                                                           ident[0:TT, 0:TT])
                        last.then_inc(S["SPT_done"], 1)

                    def body(i, par, uses):
                        here, one, two = stages(i)
                        if not (isinstance(i, int) and i >= NU - 1):
                            project(i + 1, 1 - par, uses + par)
                        if not (isinstance(i, int) and i >= NU - 2):
                            turn_context(i + 2, par, uses + 1)
                        if one:
                            gate(i - 1)
                        if two:
                            gather(i - 2, par)
                            turn_slots(i - 2)
                        if one:
                            spread(i - 1)
                        if here:
                            pe.wait_ge(S["x2_done"], i + 1)
                            pe.wait_ge(S["x2T_copied"], i)
                            for h in range(KD):
                                for u in range(2):
                                    last = nc.tensor.transpose(x2T_ps[:, h * UT + u * TT:h * UT + (u + 1) * TT],
                                                               x2[par][:, u, h * P:(h + 1) * P], ident[0:TT, 0:TT])
                            last.then_inc(S["x2T_done"], 1)
                    turn_context(0, 0, 1)
                    turn_context(1, 1, 1)
                    project(0, 0, 1)
                    over_stages(pe, body)

        s_l1, s_gelu, s_y, s_yc = sem("l1_done"), sem("gelu_done"), sem("y_done"), sem("y_copied")
        s_w1h, s_w1l, s_w2h, s_w2l = sem("w1_hi"), sem("w1_lo"), sem("w2_hi"), sem("w2_lo")
        s_xh, s_xl, s_hh, s_hl = sem("xin_hi"), sem("xin_lo"), sem("hidden_hi"), sem("hidden_lo")
        HS = SLOTS // 2
        QW = KD * HID // 4
        PARTS = ((0, 0), (0, 1), (1, 0))
        with ExitStack() as ctx:
            def sbr(name, shape):
                return ctx.enter_context(nc.sbuf_tensor(name, shape, F32R))
            w1p = [sbr("w1_hi_s", [P, KD, HID]), sbr("w1_lo_s", [P, KD, HID])]
            w2p = [sbr("w2_hi_s", [P, KH, D]), sbr("w2_lo_s", [P, KH, D])]
            xp = [sbr("xin_hi_s", [P, KD, SLOTS]), sbr("xin_lo_s", [P, KD, SLOTS])]
            hp = [sbr("hidden_hi_s", [P, KH, SLOTS]), sbr("hidden_lo_s", [P, KH, SLOTS])]
            hf = [sb(ctx, f"hidden{k}", [P, HS]) for k in range(4)]

            def quarter(t, q):
                return t[:].rearrange("p k n -> p (k n)")[:, q * QW:(q + 1) * QW]

            with nc.Block() as block:
                def experts(eng, body):
                    body(0)
                    with eng.Fori(1, E - 1) as e:
                        body(e)
                    body(E - 1)

                def final(e):
                    return isinstance(e, int) and e == E - 1

                @block.sync
                def _(sp):
                    with sp.Fori(1, E) as e:
                        sp.wait_ge(s_w1l, e * 4)
                        sp.dma_start(w1s[:], w1[bass.ds(e, 1)].rearrange("o (k p) n -> p (o k) n", p=P)).then_inc(s_w1, 16)
                        sp.wait_ge(s_w2l, e * KH)
                        sp.dma_start(w2s[:], w2[bass.ds(e, 1)].rearrange("o (k p) n -> p (o k) n", p=P)).then_inc(s_w2, 16)

                @block.tensor
                def _(pe):
                    def body(e):
                        for m in range(KH):
                            if m == 0:
                                pe.wait_ge(s_w1l, (e + 1) * 4)
                                pe.wait_ge(s_xl, e + 1)
                            for n in range(2):
                                j = (2 * m + n) % 4
                                if not (isinstance(e, int) and e == 0 and 2 * m + n < 4):
                                    pe.wait_ge(s_gelu, e * 16 + 2 * m + n - 3)
                                for k in range(KD):
                                    for a, b in PARTS:
                                        last = nc.tensor.matmul(bank[j][:, 0:HS], w1p[a][:, k, m * P:(m + 1) * P],
                                                                xp[b][:, k, n * HS:(n + 1) * HS],
                                                                start=(k == 0 and (a, b) == PARTS[0]),
                                                                stop=(k == KD - 1 and (a, b) == PARTS[-1]))
                                last.then_inc(s_l1, 1)
                        pe.wait_ge(s_w2l, (e + 1) * KH)
                        for f in range(KD):
                            for n in range(2):
                                pe.wait_ge(s_yc, e * 4)
                                for m in range(KH):
                                    if f == 0:
                                        pe.wait_ge(s_hl, e * 16 + 2 * m + n + 1)
                                    for a, b in PARTS:
                                        last = nc.tensor.matmul(bank[4 + 2 * f + n][:, 0:HS], w2p[a][:, m, f * P:(f + 1) * P],
                                                                hp[b][:, m, n * HS:(n + 1) * HS],
                                                                start=(m == 0 and (a, b) == PARTS[0]),
                                                                stop=(m == KH - 1 and (a, b) == PARTS[-1]))
                                last.then_inc(s_y, 1)
                    experts(pe, body)

                @block.scalar
                def _(act):
                    def high_w1(e):
                        act.wait_ge(s_w1, (e + 1) * 16)
                        act.wait_ge(s_l1, e * 16)
                        for q in range(4):
                            nc.scalar.activation(quarter(w1p[0], q), quarter(w1s, q), ACT.Copy).then_inc(s_w1h, 1)

                    def body(e):
                        act.wait_ge(s_w2, (e + 1) * 16)
                        act.wait_ge(s_y, e * 4)
                        for m in range(KH):
                            nc.scalar.activation(w2p[0][:, m], w2s[:, m], ACT.Copy).then_inc(s_w2h, 1)
                            for n in range(2):
                                i = 2 * m + n
                                act.wait_ge(s_l1, e * 16 + i + 1)
                                if not (isinstance(e, int) and e == 0 and i < 4):
                                    act.wait_ge(s_hl, e * 16 + i - 3)
                                nc.scalar.activation(hf[i % 4][:], bank[i % 4][:, 0:HS], ACT.Gelu).then_inc(s_gelu, 1)
                        if not final(e):
                            high_w1(e + 1)
                    high_w1(0)
                    experts(act, body)

                @block.gpsimd
                def _(pool):
                    def low_w1(e):
                        for q in range(4):
                            pool.wait_ge(s_w1h, e * 4 + q + 1)
                            nc.gpsimd.tensor_tensor(quarter(w1p[1], q), quarter(w1s, q), quarter(w1p[0], q),
                                                    ALU.subtract).then_inc(s_w1l, 1)

                    def body(e):
                        for m in range(KH):
                            pool.wait_ge(s_w2h, e * KH + m + 1)
                            nc.gpsimd.tensor_tensor(w2p[1][:, m], w2s[:, m], w2p[0][:, m], ALU.subtract).then_inc(s_w2l, 1)
                        if not final(e):
                            low_w1(e + 1)
                    low_w1(0)
                    experts(pool, body)

                @block.vector
                def _(dve):
                    def split_tokens(e):
                        src = xinT[:, :, e, 0:SLOTS] if isinstance(e, int) else xinT[:, :, bass.ds(e, 1), 0:SLOTS]
                        def part(k):
                            return xp[k][:] if isinstance(e, int) else xp[k][:].unsqueeze(2)
                        dve.wait_ge(s_l1, e * 16)
                        nc.vector.tensor_copy(part(0), src).then_inc(s_xh, 1)
                        dve.wait_ge(s_xh, e + 1)
                        nc.vector.tensor_tensor(part(1), src, part(0), ALU.subtract).then_inc(s_xl, 1)

                    def part_of(k, i):
                        return hp[k][:, i // 2, i % 2 * HS:(i % 2 + 1) * HS]

                    def body(e):
                        dve.wait_ge(s_y, e * 4)
                        for i in range(17):
                            if i < 16:
                                dve.wait_ge(s_gelu, e * 16 + i + 1)
                                nc.vector.tensor_copy(part_of(0, i), hf[i % 4][:]).then_inc(s_hh, 1)
                            if i > 0:
                                dve.wait_ge(s_hh, e * 16 + i)
                                nc.vector.tensor_tensor(part_of(1, i - 1), hf[(i - 1) % 4][:], part_of(0, i - 1),
                                                        ALU.subtract).then_inc(s_hl, 1)
                        if not final(e):
                            split_tokens(e + 1)
                        for f in range(KD):
                            for n in range(2):
                                dve.wait_ge(s_y, e * 4 + 2 * f + n + 1)
                                nc.vector.tensor_copy(xinT[:, f, bass.ds(e, 1), n * HS:(n + 1) * HS],
                                                      bank[4 + 2 * f + n][:, 0:HS].unsqueeze(1)).then_inc(s_yc, 1)
                    split_tokens(0)
                    experts(dve, body)

        s_spt = [sem("spt_in0"), sem("spt_in1")]
        s_ys, s_yt, s_ysl, s_comb, s_out = sem("y_gathered"), sem("y_turned"), sem("y_slots"), sem("combined"), sem("summed")
        s_ost = [sem("out_stored0"), sem("out_stored1")]
        with ExitStack() as ctx:
            spt = [sb(ctx, f"spt{k}", [TT, 2, 2 * TT]) for k in range(2)]
            ys = [sb(ctx, f"ys{k}", [P, 2, KD, E, TS]) for k in range(2)]
            ysl = [sb(ctx, f"ysl{k}", [TT, 2, 2, D]) for k in range(2)]
            os_ = [sb(ctx, f"os{k}", [TT, 2, D]) for k in range(2)]
            YT, CB = (bank[0:2], bank[2:4]), bank[4:6]
            with nc.Block() as block:
                @block.sync
                def _(sp):
                    def load(i, par):
                        sp.dma_start(spt[par][:], spt_d[bass.ds(i * 2, 2)].rearrange("u p n -> p u n")).then_inc(s_spt[par], 16)
                    load(0, 0)
                    load(1, 1)
                    rows = out.rearrange("b n e -> (b n) e")

                    def body(i, par, uses):
                        sp.wait_ge(s_comb, i + 1)
                        if not (isinstance(i, int) and i >= NU - 2):
                            load(i + 2, par)
                        sp.wait_ge(s_out, i + 1)
                        if isinstance(i, int) and i == NU - 1:
                            t0 = i * UT
                            sp.dma_start(rows[t0:t0 + TT, :], os_[par][:, 0, :]).then_inc(s_ost[par], 16)
                            left = B * N - t0 - TT
                            sp.dma_start(rows[t0 + TT:t0 + TT + left, :], os_[par][0:left, 1, :]).then_inc(s_ost[par], 16)
                        else:
                            sp.dma_start(rows[bass.ds(i * UT, UT), :].rearrange("(u t) e -> t u e", u=2), os_[par][:]).then_inc(s_ost[par], 16)
                    over_units(sp, body)
                    sp.wait_ge(s_ost[0], (NU + 1) // 2 * 16 + 16)
                    sp.wait_ge(s_ost[1], NU // 2 * 16)

                @block.gpsimd
                def _(pool):
                    def body(i, par, uses):
                        if not (isinstance(i, int) and i < 2):
                            pool.wait_ge(s_yt, i - 1)
                        for u in range(2):
                            for f in range(KD):
                                last = nc.gpsimd.tensor_copy(ys[par][:, u, f], xinT[:, f, :, bass.ds((i * 2 + u) * TS, TS)])
                        last.then_inc(s_ys, 1)
                    over_units(pool, body)

                @block.tensor
                def _(pe):
                    def turn(i, par):
                        pe.wait_ge(s_ys, i + 1)
                        if not (isinstance(i, int) and i < 2):
                            pe.wait_ge(s_ysl, (i - 1) * 2)
                        for u in range(2):
                            for q in range(2):
                                for f in range(KD):
                                    last = nc.tensor.transpose(YT[par][u][0:TT, q * D + f * P:q * D + (f + 1) * P],
                                                               ys[par][:, u, f, 4 * q:4 * q + 4, :].rearrange("p e s -> p (e s)"), ident)
                        last.then_inc(s_yt, 1)

                    def body(i, par, uses):
                        if not (isinstance(i, int) and i == NU - 1):
                            turn(i + 1, 1 - par)
                        pe.wait_ge(s_ysl, (i + 1) * 2)
                        pe.wait_ge(s_spt[par], uses * 16)
                        if not (isinstance(i, int) and i < 2):
                            pe.wait_ge(s_out, i - 1)
                        for u in range(2):
                            for q in range(2):
                                last = nc.tensor.matmul(CB[par][0:TT, u * D:(u + 1) * D], spt[par][:, u, q * TT:(q + 1) * TT],
                                                        ysl[par][:, u, q, :], start=(q == 0), stop=(q == 1))
                        last.then_inc(s_comb, 1)
                    turn(0, 0)
                    over_units(pe, body)

                @block.scalar
                def _(act):
                    def body(i, par, uses):
                        act.wait_ge(s_yt, i + 1)
                        if not (isinstance(i, int) and i < 2):
                            act.wait_ge(s_comb, i - 1)
                        for u in range(2):
                            nc.scalar.activation(ysl[par][:, u], YT[par][u][0:TT, :].rearrange("p (q e) -> p q e", q=2),
                                                 ACT.Copy).then_inc(s_ysl, 1)
                    over_units(act, body)

                @block.vector
                def _(dve):
                    def body(i, par, uses):
                        dve.wait_ge(s_comb, i + 1)
                        dve.wait_ge(s_ost[par], (uses - 1) * 16)
                        nc.vector.tensor_tensor(os_[par][:], CB[par][0:TT, :].rearrange("p (u e) -> p u e", u=2),
                                                hb[:, bass.ds(i * 2, 2), :], ALU.add).then_inc(s_out, 1)
                    over_units(dve, body)


_INS = ['x', 'L0_tok_W', 'L0_tok_b', 'L0_attn_wq', 'L0_attn_bq', 'L0_attn_wk', 'L0_attn_bk', 'L0_attn_wv', 'L0_attn_bv',
        'L0_attn_wo', 'L0_attn_bo', 'L0_attn_gamma', 'L0_attn_beta', 'L0_ffn_gate_w', 'L0_ffn_w1', 'L0_ffn_w2']


def kernel(**inputs):
    import concourse.bacc as _bacc
    from concourse.bass_utils import run_bass_kernel_spmd as _run

    nc = _bacc.Bacc("TRN2", target_bir_lowering=False, num_devices=1)
    arrays, args = {}, []
    for name in _INS:
        a = np.ascontiguousarray(inputs[name])
        arrays[f"in_{name}"] = a
        args.append(nc.dram_tensor(f"in_{name}", a.shape, mybir.dt.from_np(a.dtype), kind="ExternalInput").ap())
    arrays["in_masks"] = shape_masks()
    args.append(nc.dram_tensor("in_masks", arrays["in_masks"].shape, F32, kind="ExternalInput").ap())
    args.append(nc.dram_tensor("out_0", (B, N, D), F32, kind="ExternalOutput").ap())
    build(nc, *args)
    r = _run(nc, [arrays], core_ids=[0])
    return r.results[0]["out_0"]
```

```python
from contextlib import ExitStack

import numpy as np

import concourse.bass as bass
from concourse import mybir

F32 = mybir.dt.float32
F32R = mybir.dt.float32r
PARTS = ((0, 0), (0, 1), (1, 0))
ALU = mybir.AluOpType
ACT = mybir.ActivationFunctionType
AX = mybir.AxisListType.X

P = 128
B, C, IMG, PATCH = 64, 3, 96, 16
G = IMG // PATCH
N = G * G
D = 256
KD = D // P
KF = C * PATCH * PATCH // P
HEADS, HD = 16, 16
E, CAP = 8, 2 * N // 8
HID = 1024
KH = HID // P
UB = 6
UT = UB * N
NU = -(-B // UB)
LASTB = B - (NU - 1) * UB
TT = 3 * N
T = NU * UT
SLOTS = B * CAP
PSLOTS = NU * UB * CAP
TS = 3 * CAP
LN_EPS = 1e-5

M_ID = 0
M_BLK = M_ID + P
M_I36 = M_BLK + TT
M_LOW = M_I36 + N
M_IOTA = M_LOW + N
M_M8 = M_IOTA + TS
M_A3 = M_M8 + 8
M_END = M_A3 + 3
AB = 8
AU = B // AB
AI = HEADS // 2
CST = 2 * 16


def shape_masks():
    m = np.zeros((P, M_END), np.float32)
    t = np.arange(TT)
    m[:, M_ID:M_ID + P] = np.eye(P)
    m[:TT, M_BLK:M_BLK + TT] = (t[:, None] // N) == (t[None, :] // N)
    m[:TT, M_I36:M_I36 + N] = (t[:, None] % N) == np.arange(N)[None, :]
    m[:TT, M_LOW:M_LOW + N] = np.arange(N)[None, :] < (t[:, None] % N)
    s = np.arange(TS)
    m[:TT, M_IOTA:M_IOTA + TS] = np.where(s[None, :] // CAP == t[:, None] // N, s[None, :] % CAP, -1)
    m[:, M_M8:M_M8 + AB] = np.arange(P)[:, None] // HD == np.arange(AB)[None, :]
    m[:TT, M_A3:M_A3 + 3] = (t[:, None] // N) == np.arange(3)[None, :]
    return m


def over_units(eng, body, units=NU):
    for i in range(2):
        body(i, i, 1)
    pairs = (units - 4) // 2
    with eng.Fori(0, pairs) as p:
        body(p * 2 + 2, 0, p + 2)
        body(p * 2 + 3, 1, p + 2)
    for i in range(2 * pairs + 2, units):
        body(i, i % 2, i // 2 + 1)


def last_unit(i):
    return isinstance(i, int) and i == NU - 1


def build(nc, x, tok_w, tok_b, wq, bq, wk, bk, wv, bv, wo, bo, gamma, beta, gate_w, w1, w2, masks, out):
    def dram(name, shape):
        return nc.dram_tensor(name, shape, F32).ap()

    q_d = dram("q_scratch", [NU * UB, D, N])
    k_d = dram("k_scratch", [NU * UB, D, N])
    v_d = dram("v_scratch", [T, D])
    c_d = dram("c_scratch", [T, D])
    spt_d = dram("spt_scratch", [NU * 2, TT, 2 * TT])
    q_store, k_store = (t.rearrange("b (h p) t -> h p b t", p=P) for t in (q_d, k_d))
    q_load, k_load = (t.rearrange("b (d j) t -> (b d) (j t)", d=HD) for t in (q_d, k_d))
    c_view = c_d[0:B * N, :].rearrange("t e -> (t e)").rearrange("(b m h q d) -> h q (b m) d", b=B, h=2, q=N, d=HD)
    v_flat = v_d.rearrange("t e -> (t e)")

    top = ExitStack()
    with top:
        def sem(name):
            return top.enter_context(nc.semaphore(name))

        def sb(ctx, name, shape):
            return ctx.enter_context(nc.sbuf_tensor(name, shape, F32))

        def sbr(ctx, name, shape):
            return ctx.enter_context(nc.sbuf_tensor(name, shape, F32R))

        def parts(ctx, name, shape):
            return [sbr(ctx, name + "_hi", shape), sbr(ctx, name + "_lo", shape)]

        def psum(ctx, name):
            return ctx.enter_context(nc.psum_tensor(name, [P, 512], F32))

        bank = [psum(top, f"bank{i}") for i in range(8)]
        mk = sb(top, "mk", [P, M_END])
        ident = mk[:, M_ID:M_ID + P]
        colb = sb(top, "colb", [P, 2, KD])
        rowb = sb(top, "rowb", [TT, 5, D])
        wo_s = sb(top, "wo_s", [P, KD, D])
        gate_s = sb(top, "gate_s", [P, KD, E])
        nh = sb(top, "nh", [TT, 2])
        hb = sb(top, "hb", [TT, 2 * NU, D])
        x1b = sb(top, "x1b", [TT, 2 * NU, D])
        s_const = sem("const_in")

        s_parted = sem("waits_parted")

        def part_waits(eng):
            eng.sem_inc(s_parted, 1)

        bv_bc, bo_bc, ga_bc, be_bc, tb_bc = (rowb[:, k, :] for k in range(5))

        def two(ap):
            return ap.unsqueeze(1).to_broadcast([TT, 2, D])

        s_wts = sem("weights_in")
        WTS = 14
        s_x = [sem("x_in0"), sem("x_in1")]
        s_wTt, s_wTc = sem("wT_transposed"), sem("wT_copied")
        s_hve = sem("h_var_eps")
        s_nh = sem("minus_half")
        s_xr = sem("pixels_regrouped")
        s_pT, s_pTc = sem("patches_transposed"), sem("patches_copied")
        s_hP = sem("h_product_done")
        s_h, s_hbn, s_hag, s_hrs, s_x1, s_hb = (sem(n) for n in ("h_done", "h_bn", "h_aggr", "h_rstd", "x1_done", "hb_done"))
        s_x1b = sem("x1b_done")
        s_x1T, s_x1Tc = sem("x1T_done"), sem("x1T_copied")
        s_qk, s_qkc, s_v, s_vc = sem("qk_done"), sem("qk_copied"), sem("v_done"), sem("v_copied")
        s_qkst, s_vst = sem("qk_stored"), sem("v_stored")
        s_wTl, s_pTl, s_x1Tl = sem("wT_low"), sem("patches_low"), sem("x1T_low")
        s_bq4, s_wp = sem("bq_scaled"), sem("weights_permuted")

        cs = [sb(top, f"cs{k}", [P, AB, AI, HD]) for k in range(2)]
        cN = [sb(top, f"cN{k}", [TT, 2, D]) for k in range(2)]
        s_c_in = [sem("ctx_in0"), sem("ctx_in1")]
        stage = ExitStack()
        qs = sb(stage, "qs", [P, KD, UT])
        ks = sb(stage, "ks", [P, KD, UT])
        vs = sb(stage, "vs", [TT, 2, D])
        qst = [sb(stage, f"qst{k}", [P, HEADS, N]) for k in range(2)]
        kst = [sb(stage, f"kst{k}", [P, HEADS, N]) for k in range(2)]
        vb = [sb(stage, f"vb{k}", [TT, 3, HEADS, 3, HD + 1]) for k in range(2)]
        Qc = [sb(stage, f"Qc{k}", [P, HEADS * N]) for k in range(2)]
        Kbd0 = sb(stage, "Kbd0", [P, HEADS, AB, N])
        Kc = sb(stage, "Kc", [P, HEADS * N])
        SC, PT, PV = bank[0:4], bank[6:8], bank[4:6]
        s_q_in = [sem("qk_in0"), sem("qk_in1")]
        s_v_in = [sem("v_in0"), sem("v_in1")]
        s_z, s_one, s_zb, s_pad = sem("values_zeroed"), sem("value_ones"), sem("banks_zeroed"), sem("padding_zeroed")
        s_Qc, s_Kc, s_Kbd = sem("Q_ordered"), sem("K_ordered"), sem("K_blocked")
        s_S, s_red, s_sub, s_exp = sem("scores_done"), sem("max_done"), sem("max_subtracted"), sem("exp_done")
        s_T, s_Tc, s_PV, s_rc, s_ctx = sem("probs_turned"), sem("probsT_copied"), sem("PV_done"), sem("rec_done"), sem("ctx_done")
        s_cst = [sem("ctx_stored0"), sem("ctx_stored1")]


        def load_qk(sp, i, par):
            for dst, src in ((qst, q_load), (kst, k_load)):
                sp.dma_start(dst[par][:].rearrange("p j t -> p (j t)"), src[bass.ds(i * P, P), :]).then_inc(s_q_in[par], 16)

        def load_v(sp, i, par):
            for s in range(AB):
                t0 = (i * AB + s) * N
                src = v_flat[bass.ds(t0 * D, N * D)].rearrange("(g k d) -> k g d", k=N, d=HD)
                r0 = s % 3 * N
                sp.dma_start(vb[par][r0:r0 + N, s // 3, :, s % 3, 0:HD], src).then_inc(s_v_in[par], 16)

        def order(dve, i, par, uses):
            dve.wait_ge(s_q_in[par], uses * 2 * 16)
            dve.wait_ge(s_Kbd, i * 4)
            nc.vector.tensor_copy(Kc[:].rearrange("p (t j) -> p t j", j=HEADS),
                                  kst[par][:].rearrange("p j t -> p t j")).then_inc(s_Kc, 1)
            if not (isinstance(i, int) and i < 2):
                dve.wait_ge(s_S, (i - 1) * AI)
            nc.vector.tensor_copy(Qc[par][:].rearrange("p (t j) -> p t j", j=HEADS),
                                  qst[par][:].rearrange("p j t -> p t j")).then_inc(s_Qc, 1)

        def block_keys(Kbd, quarters=range(4)):
            mask = mk[:, M_M8:M_M8 + AB].unsqueeze(1).unsqueeze(3).to_broadcast([P, 4, AB, N])
            kg = Kc[:].rearrange("p (g k) -> p g k", k=N)
            for q in quarters:
                nc.gpsimd.tensor_tensor(Kbd[:, 4 * q:4 * q + 4], mask,
                                        kg[:, 4 * q:4 * q + 4, :].unsqueeze(2).to_broadcast([P, 4, AB, N]),
                                        ALU.mult).then_inc(s_Kbd, 1)

        def load_contexts(sp, i, par):
            src = c_d[bass.ds(i * UT, UT), :].rearrange("(u t) e -> t u e", u=2)
            sp.dma_start(cN[par][:], src).then_inc(s_c_in[par], 16)

        def store_projected(sp, j):
            sp.wait_ge(s_vc, j + 1)
            sp.wait_ge(s_qkc, j * 4 + 4)
            part_waits(sp)
            sp.dma_start(v_d[bass.ds(j * UT, UT), :].rearrange("(u t) e -> t u e", u=2), vs[:]).then_inc(s_vst, 16)
            for dst, src in ((q_store, qs), (k_store, ks)):
                for h in range(KD):
                    sp.dma_start(dst[h][:, bass.ds(j * UB, UB), :],
                                 src[:, h, :].rearrange("p (b t) -> p b t", t=N)).then_inc(s_qkst, 16)

        def store_contexts(sp, i, par):
            sp.wait_ge(s_ctx, (i + 1) * AI)
            part_waits(sp)
            for h in range(2):
                sp.dma_start(c_view[h][:, bass.ds(i * AB * AI, AB * AI), :],
                             cs[par][64 * h:64 * h + N].rearrange("p s m d -> p (s m) d")).then_inc(s_cst[par], 16)

        with ExitStack() as ctx, nc.allow_non_contiguous_dma(reason="bias columns"):
            XP = C * UB * G
            xraw = [sb(ctx, f"xraw{k}", [XP, PATCH * IMG]) for k in range(2)]
            xr = sb(ctx, "xr", [XP, G, PATCH * PATCH])
            wnat = sb(ctx, "wnat", [P, KD, C * PATCH * PATCH])
            wT = parts(ctx, "wT", [P, KF, D])
            wq_s, wk_s, wv_s = (sb(ctx, n, [P, KD, D]) for n in ("wq_s", "wk_s", "wv_s"))
            wq_p, wk_p, wv_p = (parts(ctx, n, [P, KD, D]) for n in ("wq_p", "wk_p", "wv_p"))
            pT = parts(ctx, "pT", [P, KF, UT])
            hs = sb(ctx, "hs", [TT, 2, D])
            x1s = sb(ctx, "x1s", [TT, 2, D])
            x1Ts = parts(ctx, "x1Ts", [P, KD, UT])
            st = sb(ctx, "st", [TT, 2, 6])
            mv = sb(ctx, "mv", [TT, 2, 2])
            rs = sb(ctx, "rs", [TT, 2])
            ve = sb(ctx, "ve", [TT, 2])

            def patch_block(q, gg):
                src = bank[q][:, gg * 2 * XP:(gg + 1) * 2 * XP].rearrange("p (f c r) -> p f c r", f=2, c=C)
                dst = [t[:].rearrange("p (c f) (r g) -> p g f c r", c=C, g=G)[:, 2 * q + gg] for t in pT]
                return src, dst

            h_ps, x1T_ps, q_ps, k_ps, v_ps = bank[4], bank[5], bank[6], bank[7], bank[5]

            with nc.Block() as block:
                @block.sync
                def _(sp):
                    def load_x(i, par):
                        nb = LASTB if isinstance(i, int) and i == NU - 1 else UB
                        for c in range(C):
                            src = x[bass.ds(i * UB, nb), c, :, :].rearrange("b (g r) w -> b g (r w)", g=G)
                            sp.dma_start(xraw[par][c * UB * G:c * UB * G + nb * G, :], src).then_inc(s_x[par], 16)

                    sp.dma_start(wnat[:], tok_w.rearrange("(h p) f -> p h f", p=P)).then_inc(s_const, 16)
                    sp.dma_start(mk[:], masks).then_inc(s_const, 16)
                    load_x(0, 0)
                    load_x(1, 1)
                    for k, v in ((0, bq), (1, bk)):
                        for h in range(KD):
                            src = v.rearrange("(j h d o) -> h d j o", h=KD, d=HD // KD, o=1)[h]
                            sp.dma_start(colb[:, k, h:h + 1], src).then_inc(s_wts, 16)
                    for k, v in enumerate((bv, bo, gamma, beta, tok_b)):
                        sp.dma_start(rowb[:, k, :], v.partition_broadcast(TT)).then_inc(s_wts, 16)
                    for dst, v in ((wq_s, wq), (wk_s, wk), (wv_s, wv), (wo_s, wo), (gate_s, gate_w)):
                        sp.dma_start(dst[:], v.rearrange("(k p) n -> p k n", p=P)).then_inc(s_wts, 16)

                    def body(i, par, uses):
                        sp.wait_ge(s_xr, i + 1)
                        if not (isinstance(i, int) and i >= NU - 2):
                            load_x(i + 2, par)
                        if not (isinstance(i, int) and i == 0):
                            store_projected(sp, i - 1)
                        if isinstance(i, int) and i >= NU - 2:
                            k = i - (NU - 2)
                            sp.wait_ge(s_qkst, 64 * 3)
                            sp.wait_ge(s_vst, 16 * 3)
                            sp.wait_ge(s_one, 2)
                            load_qk(sp, k, k)
                            load_v(sp, k, k)

                    over_units(sp, body)

                @block.gpsimd
                def _(pool):
                    nc.gpsimd.memset(nh[:], -0.5).then_inc(s_nh, 1)
                    for k in range(2):
                        nc.gpsimd.memset(vb[k][:], 0.0).then_inc(s_z, 1)
                    pool.wait_ge(s_nh, 1)
                    pool.wait_ge(s_wts, WTS * 16)

                    def body(i, par, uses):
                        pool.wait_ge(s_hve, i + 1)
                        nc.gpsimd.tensor_tensor(rs[:], ve[:], nh[:], ALU.pow).then_inc(s_hrs, 1)
                        nc.gpsimd.tensor_tensor(hb[:, bass.ds(i * 2, 2), :], hs[:], two(be_bc), ALU.add).then_inc(s_hb, 1)
                        pool.wait_ge(s_x1, i + 1)
                        nc.gpsimd.tensor_tensor(x1b[:, bass.ds(i * 2, 2), :], x1s[:], two(bo_bc), ALU.add).then_inc(s_x1b, 1)
                    over_units(pool, body)
                    pool.wait_ge(s_Kc, 1)
                    block_keys(Kbd0, (0, 1))

                @block.tensor
                def _(pe):
                    pe.wait_ge(s_const, 32)
                    for k in range(KF):
                        for h in range(KD):
                            last = nc.tensor.transpose(bank[k // 2][:, (k % 2) * D + h * P:(k % 2) * D + (h + 1) * P],
                                                       wnat[:, h, k * P:(k + 1) * P], ident)
                    last.then_inc(s_wTt, 1)
                    pe.wait_ge(s_wTl, 3)

                    def patches(i, par, uses):
                        pe.wait_ge(s_xr, i + 1)
                        pe.wait_ge(s_pTl, i * 3)
                        part_waits(pe)
                        for q in range(3):
                            for n in range(4):
                                last = nc.tensor.transpose(bank[q][:, n * XP:(n + 1) * XP],
                                                           xr[:, 2 * q + n // 2, n % 2 * P:(n % 2 + 1) * P], ident[0:XP, 0:XP])
                            last.then_inc(s_pT, 1)

                    def turn_normed(j):
                        pe.wait_ge(s_x1, j + 1)
                        pe.wait_ge(s_vc, j)
                        for h in range(KD):
                            for u in range(2):
                                last = nc.tensor.transpose(x1T_ps[:, h * UT + u * TT:h * UT + (u + 1) * TT],
                                                           x1s[:, u, h * P:(h + 1) * P], ident[0:TT, 0:TT])
                        last.then_inc(s_x1T, 1)

                    def project(j):
                        if isinstance(j, int) and j == 0:
                            pe.wait_ge(s_wp, 6 * KD)
                        pe.wait_ge(s_x1Tl, j + 1)
                        for u in range(2):
                            for k in range(KD):
                                for a, b in PARTS:
                                    last = nc.tensor.matmul(v_ps[0:TT, u * D:(u + 1) * D], x1Ts[a][:, k, u * TT:(u + 1) * TT],
                                                            wv_p[b][:, k, :], start=(k == 0 and (a, b) == PARTS[0]),
                                                            stop=(k == KD - 1 and (a, b) == PARTS[-1]))
                        last.then_inc(s_v, 1)
                        pe.wait_ge(s_qkc, j * 4)
                        for w, ps in ((wq_p, q_ps), (wk_p, k_ps)):
                            for h in range(KD):
                                for k in range(KD):
                                    for a, b in PARTS:
                                        last = nc.tensor.matmul(ps[:, h * UT:(h + 1) * UT], w[a][:, k, h * P:(h + 1) * P],
                                                                x1Ts[b][:, k, :], start=(k == 0 and (a, b) == PARTS[0]),
                                                                stop=(k == KD - 1 and (a, b) == PARTS[-1]))
                            last.then_inc(s_qk, 1)

                    def body(i, par, uses):
                        lag = not (isinstance(i, int) and i == 0)
                        pe.wait_ge(s_pTl, (i + 1) * 3)
                        pe.wait_ge(s_h, i)
                        for u in range(2):
                            for k in range(KF):
                                for a, b in PARTS:
                                    last = nc.tensor.matmul(h_ps[0:TT, u * D:(u + 1) * D], pT[a][:, k, u * TT:(u + 1) * TT],
                                                            wT[b][:, k, :], start=(k == 0 and (a, b) == PARTS[0]),
                                                            stop=(k == KF - 1 and (a, b) == PARTS[-1]))
                        last.then_inc(s_hP, 1)
                        if lag:
                            turn_normed(i - 1)
                        if not last_unit(i):
                            patches(i + 1, 1 - par, uses + par)
                        if lag:
                            project(i - 1)

                    patches(0, 0, 1)
                    over_units(pe, body)
                    turn_normed(NU - 1)
                    project(NU - 1)

                @block.scalar
                def _(act):
                    act.wait_ge(s_wTt, 1)
                    for k in range(3):
                        nc.scalar.activation(wT[0][:, 2 * k:2 * k + 2, :], bank[k][:].rearrange("p (k n) -> p k n", k=2),
                                             ACT.Copy).then_inc(s_wTc, 1)

                    def patches(i):
                        for k in range(3):
                            act.wait_ge(s_pT, i * 3 + k + 1)
                            for gg in range(2):
                                src, dst = patch_block(k, gg)
                                last = nc.scalar.activation(dst[0], src, ACT.Copy)
                            last.then_inc(s_pTc, 1)

                    def copy_normed(j):
                        act.wait_ge(s_x1T, j + 1)
                        nc.scalar.activation(x1Ts[0][:], x1T_ps[:, 0:2 * UT].rearrange("p (k t) -> p k t", k=2),
                                             ACT.Copy).then_inc(s_x1Tc, 1)

                    def queries_keys(j):
                        act.wait_ge(s_qkst, j * 64)
                        for n, (dst, ps, scale) in enumerate(((qs, q_ps, HD ** -0.5), (ks, k_ps, 1.0))):
                            act.wait_ge(s_qk, j * 2 + n + 1)
                            for h in range(KD):
                                nc.scalar.activation(dst[:, h, :], ps[:, h * UT:(h + 1) * UT], ACT.Identity,
                                                     bias=colb[:, n, h:h + 1], scale=scale).then_inc(s_qkc, 1)

                    def body(i, par, uses):
                        lag = not (isinstance(i, int) and i == 0)
                        if lag:
                            copy_normed(i - 1)
                        if not last_unit(i):
                            patches(i + 1)
                        if lag:
                            queries_keys(i - 1)

                    patches(0)
                    act.wait_ge(s_wts, WTS * 16)
                    act.wait_ge(s_bq4, 1)
                    over_units(act, body)
                    copy_normed(NU - 1)
                    queries_keys(NU - 1)

                @block.vector
                def _(dve):
                    def regroup(i, par, uses):
                        dve.wait_ge(s_x[par], uses * 16 * C)
                        dve.wait_ge(s_pT, i * 3)
                        nc.vector.tensor_copy(xr[:].rearrange("p g (r w) -> p g r w", w=PATCH),
                                              xraw[par][:].rearrange("p (r g w) -> p g r w", g=G, w=PATCH)).then_inc(s_xr, 1)

                    def low_patches(i):
                        for k in range(3):
                            dve.wait_ge(s_pTc, i * 3 + k + 1)
                            for gg in range(2):
                                src, dst = patch_block(k, gg)
                                last = nc.vector.tensor_tensor(dst[1], src, dst[0], ALU.subtract)
                            last.then_inc(s_pTl, 1)

                    def low_normed(j):
                        dve.wait_ge(s_x1Tc, j + 1)
                        nc.vector.tensor_tensor(x1Ts[1][:], x1T_ps[:, 0:2 * UT].rearrange("p (k t) -> p k t", k=2),
                                                x1Ts[0][:], ALU.subtract).then_inc(s_x1Tl, 1)

                    regroup(0, 0, 1)
                    for k in range(3):
                        dve.wait_ge(s_wTc, k + 1)
                        nc.vector.tensor_tensor(wT[1][:, 2 * k:2 * k + 2, :], bank[k][:].rearrange("p (k n) -> p k n", k=2),
                                                wT[0][:, 2 * k:2 * k + 2, :], ALU.subtract).then_inc(s_wTl, 1)
                    low_patches(0)
                    regroup(1, 1, 1)
                    dve.wait_ge(s_wts, WTS * 16)
                    nc.vector.tensor_scalar(colb[:, 0, :], colb[:, 0, :], HD ** -0.5, None, ALU.mult).then_inc(s_bq4, 1)
                    count = 0
                    for k in range(KD):
                        views = [([t[:, k].rearrange("p (d j) -> p d j", d=HD) for t in dst],
                                  src[:, k].rearrange("p (j d) -> p d j", d=HD)) for dst, src in ((wq_p, wq_s), (wk_p, wk_s))]
                        views.append(([t[:, k] for t in wv_p], wv_s[:, k]))
                        for dst, src in views:
                            nc.vector.tensor_copy(dst[0], src).then_inc(s_wp, 1)
                            count += 1
                            dve.wait_ge(s_wp, count)
                            nc.vector.tensor_tensor(dst[1], src, dst[0], ALU.subtract).then_inc(s_wp, 1)
                            count += 1
                    dve.wait_ge(s_z, 2)
                    for k in range(2):
                        ones = mk[0:TT, M_A3:M_A3 + 3].unsqueeze(1).to_broadcast([TT, 3 * HEADS, 3])
                        nc.vector.tensor_copy(vb[k][:, :, :, :, HD].rearrange("p c g s -> p (c g) s"), ones).then_inc(s_one, 1)

                    def copy_values(j):
                        dve.wait_ge(s_v, j + 1)
                        dve.wait_ge(s_vst, j * 16)
                        nc.vector.tensor_tensor(vs[:], v_ps[0:TT, :].rearrange("p (u e) -> p u e", u=2), two(bv_bc),
                                                ALU.add).then_inc(s_vc, 1)

                    def body(i, par, uses):
                        if not (last_unit(i) or isinstance(i, int) and i == 0):
                            regroup(i + 1, 1 - par, uses + par)
                        dve.wait_ge(s_hP, i + 1)
                        dve.wait_ge(s_hb, i)
                        dve.wait_ge(s_x1, i)
                        nc.vector.tensor_tensor(hs[:], h_ps[0:TT, :].rearrange("p (u e) -> p u e", u=2), two(tb_bc),
                                                ALU.add).then_inc(s_h, 1)
                        if not (isinstance(i, int) and i == 0):
                            low_normed(i - 1)
                        if not last_unit(i):
                            low_patches(i + 1)
                        dve.wait_ge(s_h, i + 1)
                        for u in range(2):
                            nc.vector.bn_stats(st[:, u, :], hs[:, u, :]).then_inc(s_hbn, 1)
                        dve.wait_ge(s_hbn, (i + 1) * 2)
                        part_waits(dve)
                        for u in range(2):
                            nc.vector.bn_aggr(mv[:, u, :], st[:, u, :]).then_inc(s_hag, 1)
                        dve.wait_ge(s_hag, (i + 1) * 2)
                        nc.vector.tensor_scalar(ve[:], mv[:, :, 1], LN_EPS, None, ALU.add).then_inc(s_hve, 1)
                        if not (isinstance(i, int) and i == 0):
                            copy_values(i - 1)
                        dve.wait_ge(s_hrs, i + 1)
                        dve.wait_ge(s_x1b, i)
                        for u in range(2):
                            last = nc.vector.tensor_scalar(x1s[:, u, :], hs[:, u, :], mv[:, u, 0:1],
                                                           rs[:, u:u + 1], ALU.subtract, ALU.mult)
                        last.then_inc(s_x1, 1)
                    over_units(dve, body)
                    low_normed(NU - 1)
                    order(dve, 0, 0, 1)
                    dve.wait_ge(s_pTl, NU * 3)
                    copy_values(NU - 1)
                    dve.wait_ge(s_vc, NU)
                    for k in range(6):
                        fill = 1.0 if k in (4, 5) else 0.0
                        nc.vector.memset(bank[k][:], fill).then_inc(s_zb, 1)

        with ExitStack() as ctx:
            Kbd = [Kbd0, sb(ctx, "Kbd1", [P, HEADS, AB, N])]
            mx = [sb(ctx, f"mx{k}", [P, AB]) for k in range(4)]
            pr = [sb(ctx, f"probs{k}", [P, AB * N]) for k in range(4)]
            pT = [sb(ctx, f"probsT{k}", [TT, 3 * P]) for k in range(2)]
            rc = [sb(ctx, f"rc{k}", [P, AB]) for k in range(2)]
            pad = sb(ctx, "pad", [T - B * N, D])
            width = [TT, TT, (AB - 6) * N]

            def item(i, par, m):
                if m < AI:
                    return i, par, m
                return None if isinstance(i, int) and i == AU - 1 else (i + 1, 1 - par, m - AI)

            with nc.Block() as block:
                @block.sync
                def _(sp):
                    store_projected(sp, NU - 1)
                    sp.wait_ge(s_pad, 1)
                    sp.dma_start(c_d[B * N:T, :], pad[:]).then_inc(s_cst[0], 16)

                    def body(i, par, uses):
                        if not (isinstance(i, int) and i >= AU - 2):
                            sp.wait_ge(s_Kc, i + 1)
                            sp.wait_ge(s_Qc, i + 1)
                            if isinstance(i, int) and i == 0:
                                sp.wait_ge(s_qkst, 64 * NU)
                                sp.wait_ge(s_vst, 16 * NU)
                            load_qk(sp, i + 2, par)
                        if not (isinstance(i, int) and i >= AU - 2):
                            sp.wait_ge(s_PV, (i + 1) * AI)
                            part_waits(sp)
                            load_v(sp, i + 2, par)
                        if isinstance(i, int) and i == AU - 1:
                            sp.wait_ge(s_cst[0], CST + 16)
                            sp.wait_ge(s_cst[1], CST)
                            load_contexts(sp, 0, 0)
                            load_contexts(sp, 1, 1)
                        else:
                            store_contexts(sp, i, par)
                    over_units(sp, body, AU)

                @block.gpsimd
                def _(pool):
                    nc.gpsimd.memset(pad[:], 0.0).then_inc(s_pad, 1)
                    block_keys(Kbd0, (2, 3))

                    def body(i, par, uses):
                        if not (isinstance(i, int) and i == AU - 1):
                            pool.wait_ge(s_Kc, i + 2)
                            pool.wait_ge(s_S, i * AI)
                            block_keys(Kbd[1 - par])
                    over_units(pool, body, AU)

                @block.vector
                def _(dve):
                    def find_max(i, par, m):
                        n, b = i * AI + m, m % 4
                        dve.wait_ge(s_S, n + 1)
                        nc.vector.tensor_reduce(mx[b][:], SC[b][:, 0:AB * N].rearrange("p (s k) -> p s k", k=N), AX,
                                                ALU.max).then_inc(s_red, 1)

                    def subtract_max(i, par, m):
                        n, b = i * AI + m, m % 4
                        dve.wait_ge(s_red, n + 1)
                        if not (isinstance(n, int) and n < 4):
                            dve.wait_ge(s_T, n - 3)
                        nc.vector.tensor_tensor(pr[b][:].rearrange("p (s k) -> p s k", k=N),
                                                SC[b][:, 0:AB * N].rearrange("p (s k) -> p s k", k=N),
                                                mx[b][:].unsqueeze(2).to_broadcast([P, AB, N]), ALU.subtract).then_inc(s_sub, 1)

                    def values_of(m):
                        return PV[m % 2][:, 0:AB * (HD + 1)].rearrange("p (s d) -> p s d", d=HD + 1)

                    def invert_sums(i, par, m):
                        dve.wait_ge(s_PV, i * AI + m + 1)
                        nc.vector.reciprocal(rc[m % 2][:], values_of(m)[:, :, HD]).then_inc(s_rc, 1)

                    def context(i, par, m, uses):
                        dve.wait_ge(s_rc, i * AI + m + 1)
                        if m == 0:
                            dve.wait_ge(s_cst[par], (uses - 1) * CST + 16 * (1 - par))
                        nc.vector.tensor_tensor(cs[par][:, :, m], values_of(m)[:, :, 0:HD],
                                                rc[m % 2][:].unsqueeze(2).to_broadcast([P, AB, HD]), ALU.mult).then_inc(s_ctx, 1)

                    def body(i, par, uses):
                        for m in range(AI):
                            nxt2 = item(i, par, m + 2)
                            before = (i, par, m - 1) if m > 0 else (i - 1, 1 - par, AI - 1)
                            if isinstance(i, int) and i == 0 and m == 0:
                                before = None
                            if nxt2:
                                find_max(*nxt2)
                            if before:
                                invert_sums(*before)
                            if nxt2:
                                subtract_max(*nxt2)
                            if before:
                                context(*before, uses)
                            if m == 0 and not (isinstance(i, int) and i == AU - 1):
                                order(dve, i + 1, 1 - par, uses + par)
                    find_max(0, 0, 0)
                    find_max(0, 0, 1)
                    subtract_max(0, 0, 0)
                    subtract_max(0, 0, 1)
                    over_units(dve, body, AU)
                    invert_sums(AU - 1, (AU - 1) % 2, AI - 1)
                    context(AU - 1, (AU - 1) % 2, AI - 1, AU // 2)

                @block.scalar
                def _(act):
                    def exponent(i, par, m):
                        act.wait_ge(s_sub, i * AI + m + 1)
                        nc.scalar.activation(pr[m % 4][:], pr[m % 4][:], ACT.Exp).then_inc(s_exp, 1)

                    def copy_turned(i, par, m):
                        n = i * AI + m
                        act.wait_ge(s_T, n + 1)
                        if not (isinstance(n, int) and n < 2):
                            act.wait_ge(s_PV, n - 1)
                        nc.scalar.activation(pT[m % 2][:], PT[m % 2][0:TT, 0:3 * P], ACT.Copy).then_inc(s_Tc, 1)

                    def body(i, par, uses):
                        for m in range(AI):
                            nxt, nxt2 = item(i, par, m + 1), item(i, par, m + 2)
                            if nxt2:
                                exponent(*nxt2)
                            if nxt:
                                copy_turned(*nxt)
                    exponent(0, 0, 0)
                    exponent(0, 0, 1)
                    copy_turned(0, 0, 0)
                    over_units(act, body, AU)

                @block.tensor
                def _(pe):
                    def scores(i, par, m):
                        n, b = i * AI + m, m % 4
                        if m == 0:
                            pe.wait_ge(s_Qc, i + 1)
                        if m % 2 == 0:
                            pe.wait_ge(s_Kbd, i * 4 + m // 2 + 1)
                        if not (isinstance(n, int) and n < 4):
                            pe.wait_ge(s_sub, n - 3)
                        for h in range(2):
                            g = 2 * m + h
                            last = nc.tensor.matmul(SC[b][64 * h:64 * h + N, 0:AB * N], Qc[par][:, g * N:(g + 1) * N],
                                                    Kbd[par][:, g].rearrange("p s k -> p (s k)"), start=True, stop=True)
                        last.then_inc(s_S, 1)

                    def turn(i, par, m):
                        n, b = i * AI + m, m % 2
                        pe.wait_ge(s_exp, n + 1)
                        if not (isinstance(n, int) and n < 2):
                            pe.wait_ge(s_Tc, n - 1)
                        for c in range(3):
                            last = nc.tensor.transpose(PT[b][0:width[c], c * P:(c + 1) * P],
                                                       pr[m % 4][:, c * TT:c * TT + width[c]], ident)
                        last.then_inc(s_T, 1)

                    def values(i, par, m):
                        n, b = i * AI + m, m % 2
                        pe.wait_ge(s_Tc, n + 1)
                        if not (isinstance(n, int) and n < 2):
                            pe.wait_ge(s_ctx, n - 1)
                        for h in range(2):
                            for c in range(3):
                                w, k = width[c], width[c] // N * (HD + 1)
                                last = nc.tensor.matmul(PV[b][64 * h:64 * h + N, 51 * c:51 * c + k],
                                                        pT[b][0:w, c * P + 64 * h:c * P + 64 * h + N],
                                                        vb[par][0:w, c, 2 * m + h].rearrange("p s d -> p (s d)")[:, 0:k],
                                                        start=True, stop=True)
                        last.then_inc(s_PV, 1)

                    def body(i, par, uses):
                        for m in range(AI):
                            nxt, nxt3 = item(i, par, m + 1), item(i, par, m + 3)
                            if nxt3:
                                scores(*nxt3)
                            if nxt:
                                turn(*nxt)
                            if m == 0:
                                pe.wait_ge(s_v_in[par], uses * AB * 16)
                            values(i, par, m)
                    scores(0, 0, 0)
                    scores(0, 0, 1)
                    scores(0, 0, 2)
                    turn(0, 0, 0)
                    over_units(pe, body, AU)

        stage.close()
        names = ("c_turned c_copied o_done r_bn r_ag r_ve r_rs n1_done h2_done h2_bn h2_ag h2_ve h2_rs h2_nm x2_done "
                 "x2T_done x2T_copied g_done g_max g_sub g_exp g_sum g_rec p_done X_done Bp_done gt_done eq_done "
                 "eqL_done cnt_done rank_done S_done SP_done xin_done xin_copied SPT_done SPT_copied SPT_stored").split()
        S = {n: sem(n) for n in names}
        s_w1, s_w2 = sem("w1_in"), sem("w2_in")
        s_zy, s_low = sem("xin_zeroed"), sem("low_bf16")
        BF16 = mybir.dt.bfloat16
        SPTs = sb(top, "SPTs", [TT, 2, 2 * TT])
        xinT = sb(top, "xinT", [P, KD, E, PSLOTS])
        w1s = sb(top, "w1s", [P, KD, HID])
        w2s = sb(top, "w2s", [P, KH, D])
        s_l1 = sem("l1_done")
        s_w1h, s_w1l, s_w2h, s_w2l = sem("w1_hi"), sem("w1_lo"), sem("w2_hi"), sem("w2_lo")
        QW = KD * HID // 4
        w1p = parts(top, "w1", [P, KD, HID])

        def quarter(t, q):
            return t[:].rearrange("p k n -> p (k n)")[:, q * QW:(q + 1) * QW]

        def high_w1(act, e):
            act.wait_ge(s_w1, (e + 1) * 16)
            if not (isinstance(e, int) and e == 0):
                act.wait_ge(s_l1, e * 16)
            for q in range(4):
                nc.scalar.activation(quarter(w1p[0], q), quarter(w1s, q), ACT.Copy).then_inc(s_w1h, 1)

        def low_w1(pool, e):
            for q in range(4):
                pool.wait_ge(s_w1h, e * 4 + q + 1)
                nc.gpsimd.tensor_tensor(quarter(w1p[1], q), quarter(w1s, q), quarter(w1p[0], q),
                                        ALU.subtract).then_inc(s_w1l, 1)


        with ExitStack() as ctx:
            cT = [sb(ctx, f"cT{k}", [P, KD, UT]) for k in range(2)]
            n1 = sb(ctx, "n1", [TT, 2, D])
            x2 = [sb(ctx, f"x2_{k}", [TT, 2, D]) for k in range(2)]
            x2T = sb(ctx, "x2T", [P, KD, UT])
            stA, stB = sb(ctx, "stA", [TT, 2, 6]), sb(ctx, "stB", [TT, 2, 6])
            mvA, mvB = sb(ctx, "mvA", [TT, 2, 2]), sb(ctx, "mvB", [TT, 2, 2])
            rsA, rsB = sb(ctx, "rsA", [TT, 2]), sb(ctx, "rsB", [TT, 2])
            veA, veB = sb(ctx, "veA", [TT, 2]), sb(ctx, "veB", [TT, 2])
            nm = sb(ctx, "nm", [TT, 2])
            gm = sb(ctx, "gm", [TT, 2])
            gs = sb(ctx, "gs", [TT, 2])
            gr = sb(ctx, "gr", [TT, 2])
            ge = sb(ctx, "ge", [TT, 2, E])
            pr = [sb(ctx, f"pr{k}", [TT, 2, E]) for k in range(2)]
            X = sb(ctx, "X", [TT, 2, E, N])
            gt, eq = (ctx.enter_context(nc.sbuf_tensor(n, [TT, 2, E, N], BF16)) for n in ("gt", "eq"))
            lowb = ctx.enter_context(nc.sbuf_tensor("lowb", [TT, E, N], BF16))
            rank = sb(ctx, "rank", [TT, 2, E])
            Sm = sb(ctx, "Sm", [TT, 2, E, TS])
            SP = sb(ctx, "SP", [TT, 2, E, TS])
            o_ps, x2T_ps, cT_ps, B_ps, xin_ps, spt_ps = bank[0], bank[1], bank[2], bank[3:5], bank[5:7], bank[7]
            g_ps = spt_ps[0:TT, 4 * TT:4 * TT + 2 * E]

            def stages(i):
                return [not isinstance(i, int) or 0 <= i - k < NU for k in range(3)]

            def over_stages(eng, body, between=None):
                over_units(eng, body)
                if between:
                    between()
                body(NU, NU % 2, NU // 2 + 1)
                body(NU + 1, (NU + 1) % 2, (NU + 1) // 2 + 1)

            with nc.Block() as block:
                def halves(ap):
                    return ap.rearrange("p (u e) -> p u e", u=2)


                @block.sync
                def _(sp):
                    sp.dma_start(w1s[:], w1[0].rearrange("(k p) n -> p k n", p=P)).then_inc(s_w1, 16)
                    sp.dma_start(w2s[:], w2[0].rearrange("(k p) n -> p k n", p=P)).then_inc(s_w2, 16)

                    store_contexts(sp, AU - 1, (AU - 1) % 2)
                    sp.wait_ge(s_cst[0], AU // 2 * CST + 16)
                    sp.wait_ge(s_cst[1], (AU // 2 - 1) * CST)

                    def body(i, par, uses):
                        if isinstance(i, int) and i == 1:
                            sp.wait_ge(s_cst[1], AU // 2 * CST)
                        if not (isinstance(i, int) and i >= NU - 2):
                            sp.wait_ge(S["c_turned"], i + 1)
                            load_contexts(sp, i + 2, par)
                    over_units(sp, body)

                @block.gpsimd
                def _(pool):
                    i36 = mk[0:TT, M_I36:M_I36 + N].unsqueeze(1).to_broadcast([TT, E, N])

                    def norms(i):
                        pool.wait_ge(S["r_ve"], i + 1)
                        nc.gpsimd.tensor_tensor(rsA[:], veA[:], nh[:], ALU.pow).then_inc(S["r_rs"], 1)
                        pool.wait_ge(S["h2_ve"], i + 1)
                        pool.wait_ge(S["x2_done"], i)
                        nc.gpsimd.tensor_tensor(rsB[:], veB[:], nh[:], ALU.pow).then_inc(S["h2_rs"], 1)

                    def spreadable(j, par):
                        pool.wait_ge(S["p_done"], j + 1)
                        pool.wait_ge(S["Bp_done"], j * 2)
                        for u in range(2):
                            nc.gpsimd.tensor_tensor(X[:, u], pr[par][:, u, :].unsqueeze(2).to_broadcast([TT, E, N]), i36,
                                                    ALU.mult).then_inc(S["X_done"], 1)

                    def weighted_slots(j, par):
                        pool.wait_ge(S["SPT_done"], j)
                        for u in range(2):
                            pool.wait_ge(S["S_done"], j * 2 + u + 1)
                            nc.gpsimd.tensor_tensor(SP[:, u], Sm[:, u], pr[par][:, u, :].unsqueeze(2).to_broadcast([TT, E, TS]),
                                                    ALU.mult).then_inc(S["SP_done"], 1)

                    def body(i, par, uses):
                        here, one, two = stages(i)
                        if here:
                            norms(i)
                        if two:
                            weighted_slots(i - 2, par)
                        if one:
                            spreadable(i - 1, 1 - par)
                    over_stages(pool, body, lambda: low_w1(pool, 0))

                @block.vector
                def _(dve):
                    def stats(i, src, st, mv, ve, name, between=lambda step: None):
                        for u in range(2):
                            nc.vector.bn_stats(st[:, u, :], src[:, u, :]).then_inc(S[name + "_bn"], 1)
                        between(1)
                        dve.wait_ge(S[name + "_bn"], (i + 1) * 2)
                        part_waits(dve)
                        for u in range(2):
                            nc.vector.bn_aggr(mv[:, u, :], st[:, u, :]).then_inc(S[name + "_ag"], 1)
                        between(2)
                        dve.wait_ge(S[name + "_ag"], (i + 1) * 2)
                        nc.vector.tensor_scalar(ve[:], mv[:, :, 1], LN_EPS, None, ALU.add).then_inc(S[name + "_ve"], 1)

                    def residual(i):
                        dve.wait_ge(S["o_done"], (i + 1) * 2)
                        r = halves(o_ps[0:TT, :])
                        part_waits(dve)
                        stats(i, r, stA, mvA, veA, "r")
                        for u in range(2):
                            nc.vector.scalar_tensor_tensor(out=n1[:, u, :], in0=r[:, u, :], scalar=mvA[:, u, 0:1], in1=ga_bc,
                                                           op0=ALU.subtract, op1=ALU.mult).then_inc(S["n1_done"], 1)

                    def stream(i, between):
                        dve.wait_ge(S["r_rs"], i + 1)
                        dve.wait_ge(S["n1_done"], (i + 1) * 2)
                        for u in range(2):
                            hu = hb[:, bass.ds(i * 2 + u, 1), :].squeeze(1)
                            nc.vector.scalar_tensor_tensor(out=hu, in0=n1[:, u, :], scalar=rsA[:, u:u + 1], in1=hu,
                                                           op0=ALU.mult, op1=ALU.add).then_inc(S["h2_done"], 1)
                        between(-1)
                        dve.wait_ge(S["h2_done"], (i + 1) * 2)
                        part_waits(dve)
                        stats(i, hb[:, bass.ds(i * 2, 2), :], stB, mvB, veB, "h2", between)

                    def shift(i):
                        dve.wait_ge(S["h2_rs"], i + 1)
                        dve.wait_ge(S["x2_done"], i)
                        nc.vector.scalar_tensor_tensor(out=nm[:], in0=mvB[:, :, 0], scalar=-1.0, in1=rsB[:],
                                                       op0=ALU.mult, op1=ALU.mult).then_inc(S["h2_nm"], 1)

                    gps = g_ps.rearrange("p (u e) -> p u e", u=2)

                    def gate_max(j):
                        dve.wait_ge(S["g_done"], j + 1)
                        nc.vector.tensor_reduce(gm[:], gps, AX, ALU.max).then_inc(S["g_max"], 1)

                    def gate_subtract(j):
                        dve.wait_ge(S["g_max"], j + 1)
                        nc.vector.tensor_tensor(ge[:], gps, gm[:].unsqueeze(2).to_broadcast([TT, 2, E]),
                                                ALU.subtract).then_inc(S["g_sub"], 1)

                    def gate_sum(j):
                        dve.wait_ge(S["g_exp"], j + 1)
                        nc.vector.tensor_reduce(gs[:], ge[:], AX, ALU.add).then_inc(S["g_sum"], 1)

                    def gate_invert(j):
                        dve.wait_ge(S["g_sum"], j + 1)
                        nc.vector.reciprocal(gr[:], gs[:]).then_inc(S["g_rec"], 1)

                    def gate_probs(j, par):
                        dve.wait_ge(S["g_rec"], j + 1)
                        if not (isinstance(j, int) and j < 2):
                            dve.wait_ge(S["SP_done"], (j - 1) * 2)
                        nc.vector.tensor_tensor(pr[par][:], ge[:], gr[:].unsqueeze(2).to_broadcast([TT, 2, E]),
                                                ALU.mult).then_inc(S["p_done"], 1)

                    def compare(j, par, u, op, dst, done):
                        dve.wait_ge(S["Bp_done"], j * 2 + u + 1)
                        nc.vector.tensor_tensor(dst[:, u], B_ps[u][0:TT, 0:E * N].rearrange("p (e t) -> p e t", e=E),
                                                pr[par][:, u, :].unsqueeze(2).to_broadcast([TT, E, N]), op).then_inc(S[done], 1)

                    def count(j):
                        for u in range(2):
                            dve.wait_ge(S["eq_done"], j * 2 + u + 1)
                            nc.vector.tensor_tensor(eq[:, u], eq[:, u], lowb[:], ALU.mult).then_inc(S["eqL_done"], 1)
                        for u in range(2):
                            dve.wait_ge(S["gt_done"], j * 2 + u + 1)
                            dve.wait_ge(S["eqL_done"], j * 2 + u + 1)
                            nc.vector.tensor_tensor(gt[:, u], gt[:, u], eq[:, u], ALU.add).then_inc(S["cnt_done"], 1)

                    def rank_sum(j, u):
                        dve.wait_ge(S["cnt_done"], j * 2 + u + 1)
                        nc.vector.tensor_reduce(rank[:, u, :], gt[:, u], AX, ALU.add).then_inc(S["rank_done"], 1)

                    def slots(j, u):
                        iota = mk[0:TT, M_IOTA:M_IOTA + TS].unsqueeze(1).to_broadcast([TT, E, TS])
                        dve.wait_ge(S["xin_done"], j * 2)
                        dve.wait_ge(S["SP_done"], j * 2)
                        dve.wait_ge(S["rank_done"], j * 2 + u + 1)
                        nc.vector.tensor_tensor(Sm[:, u], rank[:, u, :].unsqueeze(2).to_broadcast([TT, E, TS]), iota,
                                                ALU.is_equal).then_inc(S["S_done"], 1)

                    def body(i, par, uses):
                        here, one, two = stages(i)
                        comparisons = [(0, ALU.is_equal, eq, "eq_done"), (0, ALU.is_gt, gt, "gt_done"),
                                       (1, ALU.is_equal, eq, "eq_done"), (1, ALU.is_gt, gt, "gt_done")]

                        def next_comparison(step=None):
                            if two:
                                compare(i - 2, par, *comparisons.pop(0))

                        if here:
                            residual(i)
                            stream(i, next_comparison)
                        while two and comparisons:
                            next_comparison()
                        if two:
                            count(i - 2)
                        if here:
                            shift(i)
                        if one:
                            gate_max(i - 1)
                        if two:
                            rank_sum(i - 2, 0)
                        if one:
                            gate_subtract(i - 1)
                        if two:
                            rank_sum(i - 2, 1)
                            slots(i - 2, 0)
                        if one:
                            gate_sum(i - 1)
                        if two:
                            slots(i - 2, 1)
                        if one:
                            gate_invert(i - 1)
                            gate_probs(i - 1, 1 - par)

                    nc.vector.memset(xinT[:, :, :, SLOTS:PSLOTS], 0.0).then_inc(s_zy, 1)
                    nc.vector.tensor_copy(lowb[:], mk[0:TT, M_LOW:M_LOW + N].unsqueeze(1).to_broadcast([TT, E, N])).then_inc(s_low, 1)
                    dve.wait_ge(s_low, 1)
                    over_stages(dve, body)

                @block.scalar
                def _(act):
                    def gate_exp(j):
                        act.wait_ge(S["g_sub"], j + 1)
                        nc.scalar.activation(ge[:], ge[:], ACT.Exp).then_inc(S["g_exp"], 1)

                    def norm(i, par):
                        act.wait_ge(S["h2_nm"], i + 1)
                        if not (isinstance(i, int) and i < 2):
                            act.wait_ge(S["xin_done"], (i - 1) * 2)
                        for u in range(2):
                            last = nc.scalar.activation(x2[par][:, u, :], hb[:, bass.ds(i * 2 + u, 1), :].squeeze(1), ACT.Identity,
                                                        bias=nm[:, u:u + 1], scale=rsB[:, u:u + 1])
                        last.then_inc(S["x2_done"], 1)

                    def gathered(j):
                        for u in range(2):
                            act.wait_ge(S["xin_done"], j * 2 + u + 1)
                            for h in range(KD):
                                last = nc.scalar.activation(xinT[:, h, :, bass.ds((j * 2 + u) * TS, TS)],
                                                            xin_ps[u][:, h * E * TS:(h + 1) * E * TS].rearrange("p (e s) -> p e s", e=E),
                                                            ACT.Copy)
                            last.then_inc(S["xin_copied"], 1)
                        act.wait_ge(S["SPT_done"], j + 1)
                        act.wait_ge(S["SPT_stored"], j * 16)
                        nc.scalar.activation(SPTs[:], spt_ps[0:TT, 0:4 * TT].rearrange("p (u n) -> p u n", u=2),
                                             ACT.Copy).then_inc(S["SPT_copied"], 1)
                        act.wait_ge(S["SPT_copied"], j + 1)
                        part_waits(act)
                        act.dma_start(spt_d[bass.ds(j * 2, 2)].rearrange("u p n -> p u n"), SPTs[:]).then_inc(S["SPT_stored"], 16)

                    def copy_context(i, par):
                        act.wait_ge(S["c_turned"], i + 1)
                        if not (isinstance(i, int) and i < 2):
                            act.wait_ge(S["o_done"], (i - 1) * 2)
                        nc.scalar.activation(cT[par][:], cT_ps[:, 0:2 * UT].rearrange("p (k t) -> p k t", k=2),
                                             ACT.Copy).then_inc(S["c_copied"], 1)

                    def body(i, par, uses):
                        here, one, two = stages(i)
                        if not (isinstance(i, int) and i >= NU - 2):
                            copy_context(i + 2, par)
                        if one:
                            gate_exp(i - 1)
                        if here:
                            norm(i, par)
                        if two:
                            gathered(i - 2)
                        if here:
                            act.wait_ge(S["x2T_done"], i + 1)
                            nc.scalar.activation(x2T[:], x2T_ps[:, 0:2 * UT].rearrange("p (k t) -> p k t", k=2),
                                                 ACT.Copy).then_inc(S["x2T_copied"], 1)
                    copy_context(0, 0)
                    copy_context(1, 1)
                    act.wait_ge(s_zy, 1)
                    over_stages(act, body, lambda: high_w1(act, 0))

                @block.tensor
                def _(pe):
                    def turn_context(i, par, uses):
                        pe.wait_ge(s_c_in[par], uses * 16)
                        pe.wait_ge(S["c_copied"], i)
                        for h in range(KD):
                            for u in range(2):
                                last = nc.tensor.transpose(cT_ps[:, h * UT + u * TT:h * UT + (u + 1) * TT],
                                                           cN[par][:, u, h * P:(h + 1) * P], ident[0:TT, 0:TT])
                        last.then_inc(S["c_turned"], 1)

                    def project(i, par, u):
                        pe.wait_ge(S["c_copied"], i + 1)
                        pe.wait_ge(S["n1_done"], i * 2)
                        for k in range(KD):
                            nc.tensor.matmul(o_ps[0:TT, u * D:(u + 1) * D], cT[par][:, k, u * TT:(u + 1) * TT],
                                             wo_s[:, k, :], start=(k == 0), stop=False)
                        nc.tensor.matmul(o_ps[0:TT, u * D:(u + 1) * D], ident[0:TT, 0:TT],
                                         x1b[:, bass.ds(i * 2 + u, 1), :].rearrange("p o e -> p (o e)"),
                                         start=False, stop=True).then_inc(S["o_done"], 1)

                    def gate(j):
                        pe.wait_ge(S["x2T_copied"], j + 1)
                        pe.wait_ge(S["g_sub"], j)
                        if not (isinstance(j, int) and j < 2):
                            pe.wait_ge(S["SPT_copied"], j - 1)
                        for u in range(2):
                            for k in range(KD):
                                last = nc.tensor.matmul(g_ps[:, u * E:(u + 1) * E], x2T[:, k, u * TT:(u + 1) * TT],
                                                        gate_s[:, k, :], start=(k == 0), stop=(k == KD - 1))
                        last.then_inc(S["g_done"], 1)

                    def spread(j):
                        pe.wait_ge(S["gt_done"], j * 2)
                        for u in range(2):
                            pe.wait_ge(S["X_done"], j * 2 + u + 1)
                            nc.tensor.matmul(B_ps[u][0:TT, 0:E * N], mk[0:TT, M_BLK:M_BLK + TT],
                                             X[:, u].rearrange("p e t -> p (e t)"), start=True, stop=True).then_inc(S["Bp_done"], 1)

                    def gather(j, par):
                        pe.wait_ge(S["xin_copied"], j * 2)
                        for u in range(2):
                            pe.wait_ge(S["S_done"], j * 2 + u + 1)
                            for h in range(KD):
                                last = nc.tensor.matmul(xin_ps[u][:, h * E * TS:(h + 1) * E * TS], x2[par][:, u, h * P:(h + 1) * P],
                                                        Sm[:, u].rearrange("p e s -> p (e s)"), start=True, stop=True)
                            last.then_inc(S["xin_done"], 1)

                    def turn_slots(j):
                        pe.wait_ge(S["SP_done"], j * 2 + 2)
                        pe.wait_ge(S["SPT_copied"], j)
                        pe.wait_ge(S["g_sub"], min(j + 2, NU) if isinstance(j, int) else j + 2)
                        for u in range(2):
                            for q in range(2):
                                last = nc.tensor.transpose(spt_ps[0:TT, (2 * u + q) * TT:(2 * u + q + 1) * TT],
                                                           SP[:, u, 4 * q:4 * q + 4, :].rearrange("p e s -> p (e s)"),
                                                           ident[0:TT, 0:TT])
                        last.then_inc(S["SPT_done"], 1)

                    def body(i, par, uses):
                        here, one, two = stages(i)
                        more = not (isinstance(i, int) and i >= NU - 1)
                        if more:
                            project(i + 1, 1 - par, 0)
                        if one:
                            gate(i - 1)
                        if more:
                            project(i + 1, 1 - par, 1)
                        if not (isinstance(i, int) and i >= NU - 2):
                            turn_context(i + 2, par, uses + 1)
                        if two:
                            gather(i - 2, par)
                            turn_slots(i - 2)
                        if one:
                            spread(i - 1)
                        if here:
                            pe.wait_ge(S["x2_done"], i + 1)
                            pe.wait_ge(S["x2T_copied"], i)
                            for h in range(KD):
                                for u in range(2):
                                    last = nc.tensor.transpose(x2T_ps[:, h * UT + u * TT:h * UT + (u + 1) * TT],
                                                               x2[par][:, u, h * P:(h + 1) * P], ident[0:TT, 0:TT])
                            last.then_inc(S["x2T_done"], 1)
                    turn_context(0, 0, 1)
                    turn_context(1, 1, 1)
                    project(0, 0, 0)
                    project(0, 0, 1)
                    over_stages(pe, body)

        s_gelu, s_y, s_yc = sem("gelu_done"), sem("y_done"), sem("y_copied")
        s_xh, s_xl, s_hh, s_hl = sem("xin_hi"), sem("xin_lo"), sem("hidden_hi"), sem("hidden_lo")
        HS = SLOTS // 2
        with ExitStack() as ctx:
            w2p = parts(ctx, "w2", [P, KH, D])
            xp = parts(ctx, "xin", [P, KD, SLOTS])
            hp = parts(ctx, "hidden", [P, KH, SLOTS])
            hf = [sb(ctx, f"hidden{k}", [P, HS]) for k in range(4)]

            with nc.Block() as block:
                def experts(eng, body):
                    body(0)
                    with eng.Fori(1, E - 1) as e:
                        body(e)
                    body(E - 1)

                def final(e):
                    return isinstance(e, int) and e == E - 1

                @block.sync
                def _(sp):
                    with sp.Fori(1, E) as e:
                        sp.wait_ge(s_w1l, e * 4)
                        sp.dma_start(w1s[:], w1[bass.ds(e, 1)].rearrange("o (k p) n -> p (o k) n", p=P)).then_inc(s_w1, 16)
                        sp.wait_ge(s_w2l, e * KH)
                        sp.dma_start(w2s[:], w2[bass.ds(e, 1)].rearrange("o (k p) n -> p (o k) n", p=P)).then_inc(s_w2, 16)
                    sp.wait_ge(S["SPT_stored"], NU * 16)

                @block.tensor
                def _(pe):
                    def body(e):
                        for m in range(KH):
                            if m == 0:
                                pe.wait_ge(s_w1l, (e + 1) * 4)
                            for n in range(2):
                                j = (2 * m + n) % 4
                                if m == 0:
                                    pe.wait_ge(s_xl, e * 2 + n + 1)
                                if not (isinstance(e, int) and e == 0 and 2 * m + n < 4):
                                    pe.wait_ge(s_gelu, e * 16 + 2 * m + n - 3)
                                for k in range(KD):
                                    for a, b in PARTS:
                                        last = nc.tensor.matmul(bank[j][:, 0:HS], w1p[a][:, k, m * P:(m + 1) * P],
                                                                xp[b][:, k, n * HS:(n + 1) * HS],
                                                                start=(k == 0 and (a, b) == PARTS[0]),
                                                                stop=(k == KD - 1 and (a, b) == PARTS[-1]))
                                last.then_inc(s_l1, 1)
                        pe.wait_ge(s_w2l, (e + 1) * KH)
                        for f in range(KD):
                            for n in range(2):
                                pe.wait_ge(s_yc, e * 4)
                                for m in range(KH):
                                    if f == 0:
                                        pe.wait_ge(s_hl, e * 16 + 2 * m + n + 1)
                                    for a, b in PARTS:
                                        last = nc.tensor.matmul(bank[4 + 2 * f + n][:, 0:HS], w2p[a][:, m, f * P:(f + 1) * P],
                                                                hp[b][:, m, n * HS:(n + 1) * HS],
                                                                start=(m == 0 and (a, b) == PARTS[0]),
                                                                stop=(m == KH - 1 and (a, b) == PARTS[-1]))
                                last.then_inc(s_y, 1)
                    experts(pe, body)

                @block.scalar
                def _(act):
                    def body(e):
                        act.wait_ge(s_w2, (e + 1) * 16)
                        act.wait_ge(s_y, e * 4)
                        for m in range(KH):
                            nc.scalar.activation(w2p[0][:, m], w2s[:, m], ACT.Copy).then_inc(s_w2h, 1)
                            for n in range(2):
                                i = 2 * m + n
                                act.wait_ge(s_l1, e * 16 + i + 1)
                                if not (isinstance(e, int) and e == 0 and i < 4):
                                    act.wait_ge(s_hl, e * 16 + i - 3)
                                nc.scalar.activation(hf[i % 4][:], bank[i % 4][:, 0:HS], ACT.Gelu).then_inc(s_gelu, 1)
                        if not final(e):
                            high_w1(act, e + 1)
                    experts(act, body)

                @block.gpsimd
                def _(pool):
                    def body(e):
                        for m in range(KH):
                            pool.wait_ge(s_w2h, e * KH + m + 1)
                            nc.gpsimd.tensor_tensor(w2p[1][:, m], w2s[:, m], w2p[0][:, m], ALU.subtract).then_inc(s_w2l, 1)
                        if not final(e):
                            low_w1(pool, e + 1)
                    experts(pool, body)

                @block.vector
                def _(dve):
                    def split_tokens(e):
                        def half(t, n):
                            return t[:, :, n * HS:(n + 1) * HS].unsqueeze(2)

                        src = [xinT[:, :, bass.ds(e, 1), n * HS:(n + 1) * HS] for n in range(2)]
                        if not (isinstance(e, int) and e == 0):
                            dve.wait_ge(s_l1, e * 16)
                        for n in range(2):
                            nc.vector.tensor_copy(half(xp[0], n), src[n]).then_inc(s_xh, 1)
                        for n in range(2):
                            dve.wait_ge(s_xh, e * 2 + n + 1)
                            nc.vector.tensor_tensor(half(xp[1], n), src[n], half(xp[0], n), ALU.subtract).then_inc(s_xl, 1)

                    def part_of(k, i):
                        return hp[k][:, i // 2, i % 2 * HS:(i % 2 + 1) * HS]

                    def body(e):
                        dve.wait_ge(s_y, e * 4)
                        for i in range(17):
                            if i < 16:
                                dve.wait_ge(s_gelu, e * 16 + i + 1)
                                nc.vector.tensor_copy(part_of(0, i), hf[i % 4][:]).then_inc(s_hh, 1)
                            if i > 0:
                                dve.wait_ge(s_hh, e * 16 + i)
                                nc.vector.tensor_tensor(part_of(1, i - 1), hf[(i - 1) % 4][:], part_of(0, i - 1),
                                                        ALU.subtract).then_inc(s_hl, 1)
                        if not final(e):
                            split_tokens(e + 1)
                        for f in range(KD):
                            for n in range(2):
                                dve.wait_ge(s_y, e * 4 + 2 * f + n + 1)
                                nc.vector.tensor_copy(xinT[:, f, bass.ds(e, 1), n * HS:(n + 1) * HS],
                                                      bank[4 + 2 * f + n][:, 0:HS].unsqueeze(1)).then_inc(s_yc, 1)
                    split_tokens(0)
                    experts(dve, body)

        s_spt = [sem("spt_in0"), sem("spt_in1")]
        s_ys, s_yt, s_ysl, s_comb, s_out = sem("y_gathered"), sem("y_turned"), sem("y_slots"), sem("combined"), sem("summed")
        s_ost = [sem("out_stored0"), sem("out_stored1")]
        with ExitStack() as ctx:
            spt = [sb(ctx, f"spt{k}", [TT, 2, 2 * TT]) for k in range(2)]
            ys = [sb(ctx, f"ys{k}", [P, 2, KD, E, TS]) for k in range(2)]
            ysl = [sb(ctx, f"ysl{k}", [TT, 2, 2, D]) for k in range(2)]
            os_ = [sb(ctx, f"os{k}", [TT, 2, D]) for k in range(2)]
            YT, CB = (bank[0:2], bank[2:4]), bank[4:6]
            with nc.Block() as block:
                @block.sync
                def _(sp):
                    def load(i, par):
                        sp.dma_start(spt[par][:], spt_d[bass.ds(i * 2, 2)].rearrange("u p n -> p u n")).then_inc(s_spt[par], 16)
                    load(0, 0)
                    load(1, 1)
                    rows = out.rearrange("b n e -> (b n) e")

                    def body(i, par, uses):
                        sp.wait_ge(s_comb, i + 1)
                        if not (isinstance(i, int) and i >= NU - 2):
                            load(i + 2, par)
                        sp.wait_ge(s_out, i + 1)
                        if isinstance(i, int) and i == NU - 1:
                            t0 = i * UT
                            sp.dma_start(rows[t0:t0 + TT, :], os_[par][:, 0, :]).then_inc(s_ost[par], 16)
                            left = B * N - t0 - TT
                            sp.dma_start(rows[t0 + TT:t0 + TT + left, :], os_[par][0:left, 1, :]).then_inc(s_ost[par], 16)
                        else:
                            sp.dma_start(rows[bass.ds(i * UT, UT), :].rearrange("(u t) e -> t u e", u=2), os_[par][:]).then_inc(s_ost[par], 16)
                    over_units(sp, body)
                    sp.wait_ge(s_ost[0], (NU + 1) // 2 * 16 + 16)
                    sp.wait_ge(s_ost[1], NU // 2 * 16)

                @block.tensor
                def _(pe):
                    def turn(i, par):
                        pe.wait_ge(s_ys, i + 1)
                        if not (isinstance(i, int) and i < 2):
                            pe.wait_ge(s_ysl, (i - 1) * 2)
                        for u in range(2):
                            for q in range(2):
                                for f in range(KD):
                                    last = nc.tensor.transpose(YT[par][u][0:TT, q * D + f * P:q * D + (f + 1) * P],
                                                               ys[par][:, u, f, 4 * q:4 * q + 4, :].rearrange("p e s -> p (e s)"), ident)
                        last.then_inc(s_yt, 1)

                    def body(i, par, uses):
                        if not (isinstance(i, int) and i == NU - 1):
                            turn(i + 1, 1 - par)
                        pe.wait_ge(s_ysl, (i + 1) * 2)
                        pe.wait_ge(s_spt[par], uses * 16)
                        if not (isinstance(i, int) and i < 2):
                            pe.wait_ge(s_out, i - 1)
                        for u in range(2):
                            for q in range(2):
                                last = nc.tensor.matmul(CB[par][0:TT, u * D:(u + 1) * D], spt[par][:, u, q * TT:(q + 1) * TT],
                                                        ysl[par][:, u, q, :], start=(q == 0), stop=(q == 1))
                        last.then_inc(s_comb, 1)
                    turn(0, 0)
                    over_units(pe, body)

                @block.scalar
                def _(act):
                    def body(i, par, uses):
                        act.wait_ge(s_yt, i + 1)
                        if not (isinstance(i, int) and i < 2):
                            act.wait_ge(s_comb, i - 1)
                        for u in range(2):
                            nc.scalar.activation(ysl[par][:, u], YT[par][u][0:TT, :].rearrange("p (q e) -> p q e", q=2),
                                                 ACT.Copy).then_inc(s_ysl, 1)
                    over_units(act, body)

                @block.vector
                def _(dve):
                    def tile_slots(i, par):
                        if not (isinstance(i, int) and i < 2):
                            dve.wait_ge(s_yt, i - 1)
                        for u in range(2):
                            for f in range(KD):
                                last = nc.vector.tensor_copy(ys[par][:, u, f], xinT[:, f, :, bass.ds((i * 2 + u) * TS, TS)])
                        last.then_inc(s_ys, 1)
                    tile_slots(0, 0)
                    tile_slots(1, 1)

                    def body(i, par, uses):
                        if not (isinstance(i, int) and i >= NU - 2):
                            tile_slots(i + 2, par)
                        dve.wait_ge(s_comb, i + 1)
                        dve.wait_ge(s_ost[par], (uses - 1) * 16)
                        nc.vector.tensor_tensor(os_[par][:], CB[par][0:TT, :].rearrange("p (u e) -> p u e", u=2),
                                                hb[:, bass.ds(i * 2, 2), :], ALU.add).then_inc(s_out, 1)
                    over_units(dve, body)


_INS = ['x', 'L0_tok_W', 'L0_tok_b', 'L0_attn_wq', 'L0_attn_bq', 'L0_attn_wk', 'L0_attn_bk', 'L0_attn_wv', 'L0_attn_bv',
        'L0_attn_wo', 'L0_attn_bo', 'L0_attn_gamma', 'L0_attn_beta', 'L0_ffn_gate_w', 'L0_ffn_w1', 'L0_ffn_w2']


def kernel(**inputs):
    import concourse.bacc as _bacc
    from concourse.bass_utils import run_bass_kernel_spmd as _run

    nc = _bacc.Bacc("TRN2", target_bir_lowering=False, num_devices=1)
    arrays, args = {}, []
    for name in _INS:
        a = np.ascontiguousarray(inputs[name])
        arrays[f"in_{name}"] = a
        args.append(nc.dram_tensor(f"in_{name}", a.shape, mybir.dt.from_np(a.dtype), kind="ExternalInput").ap())
    arrays["in_masks"] = shape_masks()
    args.append(nc.dram_tensor("in_masks", arrays["in_masks"].shape, F32, kind="ExternalInput").ap())
    args.append(nc.dram_tensor("out_0", (B, N, D), F32, kind="ExternalOutput").ap())
    build(nc, *args)
    r = _run(nc, [arrays], core_ids=[0])
    return r.results[0]["out_0"]
```
